# Optimizing a Trainium2 kernel written in Bass

```python
import numpy as np
import jax
import jax.numpy as jnp

def _softmax(x, axis=-1):
    return jax.nn.softmax(x, axis=axis)

def _gelu(x):
    return jax.nn.gelu(x, approximate=True)

def _silu(x):
    return jax.nn.silu(x)

def _sigmoid(x):
    return jax.nn.sigmoid(x)

def _layernorm(x, axis=-1, eps=1e-05):
    m = jnp.mean(x, axis=axis, keepdims=True)
    v = jnp.var(x, axis=axis, keepdims=True)
    return (x - m) / jnp.sqrt(v + eps)

def _scatter_add(tgt, idx, src, axis=0):
    return tgt.at[idx].add(src)

def _segment_sum(src, seg, n):
    return jax.ops.segment_sum(src, seg, n)
kernel_name = 'mk_flamingo_gated_d1_seqx_r8_551022'

def setup_inputs(seed: int=0):
    np.random.seed(seed)
    _w = jnp.asarray

    def _rec_inputs():
        import jax
        import jax.numpy as jnp
        _rk = jax.random.key(seed)
        x = -0.0002928 + 1 * jax.random.normal(jax.random.fold_in(_rk, 1), (32, 128, 128), jnp.float32)
        _lenS = 128 - jax.random.randint(jax.random.fold_in(_rk, 7), (32,), 0, max(1, 128 // 4) + 1, jnp.int32)
        _lenS2 = 128 - jax.random.randint(jax.random.fold_in(_rk, 8), (32,), 0, max(1, 128 // 4) + 1, jnp.int32)
        _ctx_1024P = jax.random.normal(jax.random.fold_in(_rk, 11), (32, 16, 128), jnp.float32)
        _ctx_1024c = jax.random.dirichlet(jax.random.fold_in(_rk, 511), 0.3 * jnp.ones((16,), jnp.float32), (32, 128))
        _ctx_1024t = jnp.einsum('bsk,bkd->bsd', _ctx_1024c, _ctx_1024P)
        _ctx_1024t = _ctx_1024t * jax.lax.rsqrt(jnp.mean(jnp.square(_ctx_1024t)) + 1e-12) * 0.953939
        ctx_1024 = -1.39393e-06 + 0.999914 * (_ctx_1024t + 0.3 * jax.random.normal(jax.random.fold_in(_rk, 611), (32, 128, 128), jnp.float32))
        _validS = jnp.arange(128)[None, :] < _lenS[:, None]
        _validS2 = jnp.arange(128)[None, :] < _lenS2[:, None]
        _causal = jnp.tril(jnp.ones((128, 128), dtype=bool))
        mask_BxS2_if1 = jnp.where(jnp.ones((32, 128), dtype=bool), 1, 0).astype(jnp.int32)
        _g = jax.random.normal(jax.random.fold_in(_rk, 9001), (2, 1), jnp.float32)
        _g = jnp.sign(_g) * jnp.maximum(jnp.abs(_g), 1.0) + (_g == 0) * 1.0
        g_xattn = _g[0]
        g_ffn = _g[1]
        return (x, ctx_1024, mask_BxS2_if1, g_xattn, g_ffn)
    x, ctx_1024, mask_BxS2_if1, g_xattn, g_ffn = _rec_inputs()

    def _L0_xattn_setup():
        import jax, jax.numpy as jnp
        import numpy as np
        import math
        B, S, D = (2, 256, 128)
        H = 16
        HD = D // H
        key = jax.random.key(seed)
        ks = jax.random.split(key, 12)
        scale = 1.0 / math.sqrt(D)
        inp = {'query': jax.random.normal(ks[0], (B, S, D), jnp.float32), 'key': jax.random.normal(ks[1], (B, S, D), jnp.float32), 'value': jax.random.normal(ks[2], (B, S, D), jnp.float32), 'mask': jnp.ones((B, S), jnp.int32), 'Wq': jax.random.normal(ks[3], (D, D), jnp.float32) * scale, 'bq': jnp.zeros((D,), jnp.float32), 'Wk': jax.random.normal(ks[4], (D, D), jnp.float32) * scale, 'bk': jnp.zeros((D,), jnp.float32), 'Wv': jax.random.normal(ks[5], (D, D), jnp.float32) * scale, 'bv': jnp.zeros((D,), jnp.float32), 'Wo': jax.random.normal(ks[6], (D, D), jnp.float32) * scale, 'bo': jnp.zeros((D,), jnp.float32)}
        return inp
    _L0_xattn_all = _L0_xattn_setup()
    _L0_xattn_in = {k: v for k, v in _L0_xattn_all.items() if k in ('Wq', 'bq', 'Wk', 'bk', 'Wv', 'bv', 'Wo', 'bo')}
    del _L0_xattn_all

    def _L0_ffn_setup():
        import jax, jax.numpy as jnp
        import numpy as np
        D_MODEL = 128
        HIDDEN = 512
        NUM_EXPERTS = 8
        TOP_K = 2
        NUM_SHARED = 2

        def _gelu(x):
            return jax.nn.gelu(x, approximate=False)
        key = jax.random.key(seed)
        ks = jax.random.split(key, 12)
        s = 0.02
        return {'x': jax.random.normal(ks[0], (2, 256, D_MODEL), dtype=jnp.float32), 'rW': jax.random.normal(ks[1], (D_MODEL, NUM_EXPERTS), dtype=jnp.float32) * s, 'rb': jnp.zeros((NUM_EXPERTS,), dtype=jnp.float32), 'W1': jax.random.normal(ks[2], (NUM_EXPERTS, D_MODEL, HIDDEN), dtype=jnp.float32) * s, 'b1': jnp.zeros((NUM_EXPERTS, HIDDEN), dtype=jnp.float32), 'W2': jax.random.normal(ks[3], (NUM_EXPERTS, HIDDEN, D_MODEL), dtype=jnp.float32) * s, 'b2': jnp.zeros((NUM_EXPERTS, D_MODEL), dtype=jnp.float32), 'sW1': jax.random.normal(ks[4], (NUM_SHARED, D_MODEL, HIDDEN), dtype=jnp.float32) * s, 'sb1': jnp.zeros((NUM_SHARED, HIDDEN), dtype=jnp.float32), 'sW2': jax.random.normal(ks[5], (NUM_SHARED, HIDDEN, D_MODEL), dtype=jnp.float32) * s, 'sb2': jnp.zeros((NUM_SHARED, D_MODEL), dtype=jnp.float32)}
    _L0_ffn_all = _L0_ffn_setup()
    _L0_ffn_in = {k: v for k, v in _L0_ffn_all.items() if k in ('rW', 'rb', 'W1', 'b1', 'W2', 'b2', 'sW1', 'sb1', 'sW2', 'sb2')}
    del _L0_ffn_all
    return {'x': x, 'ctx_1024': ctx_1024, 'mask_BxS2_if1': mask_BxS2_if1, 'g_xattn': g_xattn, 'g_ffn': g_ffn, 'L0_xattn_Wq': _L0_xattn_in['Wq'], 'L0_xattn_bq': _L0_xattn_in['bq'], 'L0_xattn_Wk': _L0_xattn_in['Wk'], 'L0_xattn_bk': _L0_xattn_in['bk'], 'L0_xattn_Wv': _L0_xattn_in['Wv'], 'L0_xattn_bv': _L0_xattn_in['bv'], 'L0_xattn_Wo': _L0_xattn_in['Wo'], 'L0_xattn_bo': _L0_xattn_in['bo'], 'L0_ffn_rW': _L0_ffn_in['rW'], 'L0_ffn_rb': _L0_ffn_in['rb'], 'L0_ffn_W1': _L0_ffn_in['W1'], 'L0_ffn_b1': _L0_ffn_in['b1'], 'L0_ffn_W2': _L0_ffn_in['W2'], 'L0_ffn_b2': _L0_ffn_in['b2'], 'L0_ffn_sW1': _L0_ffn_in['sW1'], 'L0_ffn_sb1': _L0_ffn_in['sb1'], 'L0_ffn_sW2': _L0_ffn_in['sW2'], 'L0_ffn_sb2': _L0_ffn_in['sb2']}

def reference(x, ctx_1024, mask_BxS2_if1, g_xattn, g_ffn, L0_xattn_Wq, L0_xattn_bq, L0_xattn_Wk, L0_xattn_bk, L0_xattn_Wv, L0_xattn_bv, L0_xattn_Wo, L0_xattn_bo, L0_ffn_rW, L0_ffn_rb, L0_ffn_W1, L0_ffn_b1, L0_ffn_W2, L0_ffn_b2, L0_ffn_sW1, L0_ffn_sb1, L0_ffn_sW2, L0_ffn_sb2):
    import jax
    import jax.numpy as jnp

    def _L0_xattn_ref(query, key, value, mask, Wq, bq, Wk, bk, Wv, bv, Wo, bo):
        import jax, jax.numpy as jnp
        import numpy as np
        import math
        B, S, D = (2, 256, 128)
        H = 16
        HD = D // H
        nb = query.shape[0]
        seq = query.shape[1]

        def proj(x, W, b):
            return (x @ W + b).reshape(nb, seq, H, HD).transpose(0, 2, 1, 3)
        q = proj(query, Wq, bq)
        k = proj(key, Wk, bk)
        v = proj(value, Wv, bv)
        scores = jnp.einsum('bhqd,bhkd->bhqk', q, k) / math.sqrt(HD)
        m = mask[:, None, None, :]
        scores = jnp.where(m == 0, jnp.float32(-10000000000.0), scores)
        p_attn = jax.nn.softmax(scores, axis=-1)
        x = jnp.einsum('bhqk,bhkd->bhqd', p_attn, v)
        x = x.transpose(0, 2, 1, 3).reshape(nb, seq, H * HD)
        return x @ Wo + bo

    def _L0_ffn_ref(x, rW, rb, W1, b1, W2, b2, sW1, sb1, sW2, sb2):
        import jax, jax.numpy as jnp
        import numpy as np
        D_MODEL = 128
        HIDDEN = 512
        NUM_EXPERTS = 8
        TOP_K = 2
        NUM_SHARED = 2

        def _gelu(x):
            return jax.nn.gelu(x, approximate=False)
        B, L, D = x.shape
        xf = x.reshape(-1, D)
        sh = _gelu(jnp.einsum('td,sdh->sth', xf, sW1) + sb1[:, None, :])
        shared = jnp.einsum('sth,shd->std', sh, sW2) + sb2[:, None, :]
        shared = shared.mean(axis=0)
        gates = xf @ rW + rb
        topk_vals, topk_idx = jax.lax.top_k(gates, TOP_K)
        topk_probs = jax.nn.softmax(topk_vals, axis=-1)
        onehot = topk_idx[:, :, None] == jnp.arange(NUM_EXPERTS)[None, None, :]
        w = jnp.sum(topk_probs[:, :, None] * onehot, axis=1)
        h = _gelu(jnp.einsum('td,edh->eth', xf, W1) + b1[:, None, :])
        y = jnp.einsum('eth,ehd->etd', h, W2) + b2[:, None, :]
        moe = jnp.einsum('te,etd->td', w, y)
        return (shared + moe).reshape(B, L, D)
    x = x + jnp.tanh(g_xattn[0]) * _L0_xattn_ref(_layernorm(x, axis=-1), ctx_1024, ctx_1024, mask_BxS2_if1, L0_xattn_Wq, L0_xattn_bq, L0_xattn_Wk, L0_xattn_bk, L0_xattn_Wv, L0_xattn_bv, L0_xattn_Wo, L0_xattn_bo)
    x = x + jnp.tanh(g_ffn[0]) * _L0_ffn_ref(_layernorm(x, axis=-1), L0_ffn_rW, L0_ffn_rb, L0_ffn_W1, L0_ffn_b1, L0_ffn_W2, L0_ffn_b2, L0_ffn_sW1, L0_ffn_sb1, L0_ffn_sW2, L0_ffn_sb2)
    return x

_drawn_inputs = setup_inputs


def setup_inputs(seed=0):
    import zlib

    import numpy as np

    out = dict(_drawn_inputs(seed))
    spreads = {'L0_xattn_bq': (0.0, 0.386),
     'L0_xattn_bk': (0.0, 0.8),
     'L0_xattn_bv': (0.0, 0.1),
     'L0_xattn_bo': (0.0, 0.1),
     'L0_ffn_rb': (0.0, 0.1),
     'L0_ffn_b1': (0.0, 0.549),
     'L0_ffn_b2': (0.0, 0.1),
     'L0_ffn_sb1': (0.0, 0.56),
     'L0_ffn_sb2': (0.0, 0.1)}
    factors = {}
    for name, (base, spread) in spreads.items():
        noise = np.random.default_rng([zlib.crc32(name.encode()), seed]).standard_normal(out[name].shape)
        drawn = base * np.exp(spread * noise) if base else spread * noise
        out[name] = jnp.asarray(drawn.astype(out[name].dtype))
    for name, factor in factors.items():
        out[name] = (out[name] * factor).astype(out[name].dtype)
    return out
```

```python
import concourse.bass as bass
from concourse import mybir
from contextlib import ExitStack

F32 = mybir.dt.float32
F16 = mybir.dt.float16
BF16 = mybir.dt.bfloat16
I32 = mybir.dt.int32
ALU = mybir.AluOpType
ACT = mybir.ActivationFunctionType
AX_X = mybir.AxisListType.X

P = 128
B, S, D = 32, 128, 128
T = B * S
NT = T // P
H, HD = 16, 8
NP = B // 2
W2T = 2 * S
E, NS = 8, 2
NE = E + NS
HID = 512
NC = HID // P
TILE = 256
NTILE = (2 * T + E * (TILE - 1)) // TILE
SLOTS = NTILE * TILE
ROW = D + 1
NOWHERE = 1 << 20
EPS = 1e-5
XN_NORM2 = 128.2
RSQRT_SEED = 0x5F3759DF
SLOT_ROWS = 4 * HD
SHIFT = 2 * SLOT_ROWS
NB = 3
BIG16 = 32768.0
SCORE_TOP = float(2 ** 29)


class Parts(dict):

    def __getattr__(self, name):
        return self[name]


def view(tile, off, *dims, parts=P, p0=0):
    full = tile[:]
    step = full.ap[0][0]
    return bass.AP(tensor=full.tensor, offset=full.offset + p0 * step + off, ap=[[step, parts], *[list(d) for d in dims]])


def wait(eng, sem, value):
    if not isinstance(value, int) or value > 0:
        eng.wait_ge(sem, value)


def settle(eng, passed):
    eng.sem_inc(passed, 1)


class Chain:

    def __init__(self, eng, sem):
        self.eng, self.sem, self.n = eng, sem, 0

    def __call__(self, ins):
        self.n += 1
        ins.then_inc(self.sem, 1)
        self.eng.wait_ge(self.sem, self.n)

    def restart(self):
        self.eng.sem_clear(self.sem)
        self.n = 0


def rsqrt(v, link, out, x, tmp, n):
    link(v.tensor_scalar(tmp.bitcast(I32), x.bitcast(I32), 1, None, ALU.arith_shift_right))
    link(v.tensor_scalar(out.bitcast(I32), tmp.bitcast(I32), -1.0, float(RSQRT_SEED), ALU.mult, ALU.add))
    for _ in range(4):
        link(v.scalar_tensor_tensor(out=tmp, in0=out, scalar=-0.5, in1=out, op0=ALU.mult, op1=ALU.mult))
        link(v.tensor_tensor(tmp, tmp, x, ALU.mult))
        link(v.scalar_tensor_tensor(out=out, in0=tmp, scalar=1.5, in1=out, op0=ALU.add, op1=ALU.mult))


def prologue(nc, io, k):
    with ExitStack() as ctx:
        sb = lambda n, s, d=F32: ctx.enter_context(nc.sbuf_tensor(n, s, d))
        sem = lambda n: ctx.enter_context(nc.semaphore(n))
        ps = lambda n, s, d=F32: ctx.enter_context(nc.psum_tensor(n, s, d))
        stage1 = sb("stage1", [P, NE * HID])
        stage2 = sb("stage2", [P, NE * HID])
        C = sb("C", [P, NT, D])
        maski = sb("maski", [P, T], I32)
        maskr = sb("maskr", [B, S], I32)
        maskf = sb("maskf", [B, S])
        b1r = sb("b1r", [NE * NC, P])
        mx = sb("mx", [P, 9])
        mxa = sb("mxa", [P, 9])
        bound = sb("bound", [P, 6])
        tmp6 = sb("tmp6", [P, 6])
        st = sb("st", [P, NT, 6])
        tmpn = sb("tmpn", [P, NT])
        tmpv = sb("tmpv", [P, NT])
        maskT = sb("maskT", [P, B])
        anyb = sb("anyb", [P, B])
        graw = sb("graw", [P, 2])
        bqk = sb("bqk", [P, 2])
        padrow = sb("padrow", [P, ROW], I32)
        constq = sb("constq", [P, W2T], F16)
        pT = ps("pT", [P, 512])
        pA = ps("pA", [P, 512])
        s_x = [sem(f"s_x{n}") for n in range(4)]
        s_c = [sem(f"s_c{n}") for n in range(4)]
        s_small, s_w1, s_w2, s_mask = sem("s_small"), sem("s_w1"), sem("s_w2"), sem("s_mask")
        s_ident, s_mx, s_mxa, s_tr, s_trc, s_any = sem("s_ident"), sem("s_mx"), sem("s_mxa"), sem("s_tr"), sem("s_trc"), sem("s_any")
        s_scale, s_whi, s_w1d, s_wlo = sem("s_scale"), sem("s_whi"), sem("s_w1d"), sem("s_wlo")
        s_dv, s_pad, s_padw, s_init, s_gl = sem("s_dv"), sem("s_pad"), sem("s_padw"), sem("s_init"), sem("s_gl")
        s_gr = sem("s_gr")
        NSMALL = 15

        with nc.Block() as block:
            @block.sync
            def _(sp):
                small = [(k.Wq[:], io.Wq), (k.Wk[:], io.Wk), (k.Wv[:], io.Wv), (k.Wo[:], io.Wo),
                         (bqk[:, 0:1], io.bq.rearrange("(p o) -> p o", o=1)), (bqk[:, 1:2], io.bk.rearrange("(p o) -> p o", o=1)),
                         (k.bv[:], io.bv.partition_broadcast(P)), (k.bo[:], io.bo.partition_broadcast(P)),
                         (k.rb[:], io.rb.partition_broadcast(P)), (k.rWf[:], io.rW),
                         (b1r[0:E * NC, :], io.b1.rearrange("e (c p) -> (e c) p", p=P)),
                         (b1r[E * NC:NE * NC, :], io.sb1.rearrange("e (c p) -> (e c) p", p=P)),
                         (k.b2[:, 0:E * D], io.b2.rearrange("e d -> (e d)").partition_broadcast(P)),
                         (k.b2[:, E * D:NE * D], io.sb2.rearrange("e d -> (e d)").partition_broadcast(P)),
                         (maskr[:], io.mask)]
                assert len(small) == NSMALL
                xv = io.x.rearrange("b s d -> s b d")
                cv = io.ctx.rearrange("b s d -> s b d")
                for n in range(4):
                    sp.dma_start(C[:, 8 * n:8 * n + 8, :], cv[:, 8 * n:8 * n + 8, :]).then_inc(s_c[n], 16)
                for dst, src in small:
                    sp.dma_start(dst, src).then_inc(s_small, 16)
                sp.dma_start(graw[:, 0:1], io.g1.partition_broadcast(P)).then_inc(s_gr, 16)
                sp.dma_start(graw[:, 1:2], io.g2.partition_broadcast(P)).then_inc(s_gr, 16)
                for n in range(4):
                    sp.dma_start(k.X[:, 8 * n:8 * n + 8, :], xv[:, 8 * n:8 * n + 8, :]).then_inc(s_x[n], 16)
                sp.dma_start(maski[:], io.mask.rearrange("b s -> (b s)").partition_broadcast(P)).then_inc(s_mask, 16)
                st4 = stage2[:].rearrange("p (e c d) -> p e c d", c=NC, d=D)
                for e in range(NE):
                    src = io.W1[e] if e < E else io.sW1[e - E]
                    sp.dma_start(stage1[:, e * HID:(e + 1) * HID], src).then_inc(s_w1, 16)
                for e in range(NE):
                    src = io.W2[e] if e < E else io.sW2[e - E]
                    sp.dma_start(st4[:, e, :, :], src.rearrange("(c p) d -> p c d", p=P)).then_inc(s_w2, 16)
                sp.wait_ge(s_init, 1)
                for u in range(NB):
                    sp.dma_start(k.scrq[u][:, 3, :], constq[:]).then_inc(s_pad, 16)
                    for par in range(2):
                        sp.dma_start(k.K[u][SHIFT + 2 * par:SHIFT + 2 * par + 2, par::2, :],
                                     constq[0:2 * HD, :]).then_inc(s_pad, 16)
                sp.wait_ge(s_pad, 3 * 16 * NB)

            @block.gpsimd
            def _(g):
                g.memset(k.identf[:], 0.0)
                g.memset(k.ident16[:], 0.0)
                g.memset(k.ones[:], 1.0)
                g.memset(k.onesb[:], 1.0)
                g.memset(k.lower[:], 1.0)
                g.memset(mx[:], 0.0)
                g.memset(constq[:], BIG16)
                g.memset(padrow[:, 0:D], 0)
                g.memset(padrow[:, D:ROW], NOWHERE)
                for u in range(NB):
                    g.memset(k.Q[u][:], 0.0)
                    g.memset(k.K[u][:], 0.0)
                    g.memset(k.V[u][:], 0.0)
                g.memset(k.onesV[:], 0.0).then_inc(s_init, 1)
                g.wait_ge(s_init, 1)
                for m in (k.identf, k.ident16):
                    g.affine_select(out=m[:], in_=m[:], compare_op=ALU.not_equal, fill=1.0, base=0,
                                    pattern=[[-1, P]], channel_multiplier=1)
                g.affine_select(out=k.lower[:], in_=k.lower[:], compare_op=ALU.is_gt, fill=0.0, base=0,
                                pattern=[[1, P]], channel_multiplier=-1)
                for i in range(4):
                    last = g.memset(k.onesV[:, i, HD * i:HD * i + HD], 1.0)
                last.then_inc(s_ident, 1)
                g.wait_ge(s_mx, 1)
                g.partition_all_reduce(mxa[:], mx[:], P, bass.bass_isa.ReduceOp.max).then_inc(s_mxa, 1)
                g.dma_start(k.xs.rearrange("(p r) w -> p r w", p=P), view(padrow, 0, [0, SLOTS // P], [1, ROW])).then_inc(s_padw, 16)
                g.wait_ge(s_padw, 16)

            @block.scalar
            def _(a):
                a.wait_ge(s_gr, 32)
                a.activation(k.gt[:], graw[:], ACT.Tanh).then_inc(s_gl, 1)
                a.wait_ge(s_scale, 1)
                for w, stg, sc in ((k.W1h, stage1, 3), (k.W2h, stage2, 4)):
                    a.activation(w[:], stg[:], ACT.Copy, scale=k.sc[:, sc:sc + 1]).then_inc(s_whi, 1)
                a.wait_ge(s_gl, 1)

            @block.tensor
            def _(t):
                t.wait_ge(s_ident, 1)
                t.wait_ge(s_small, 16 * NSMALL)
                t.transpose(pT[:, 0:NE * NC], b1r[:], k.identf[0:NE * NC, 0:NE * NC])
                t.wait_ge(s_tr, 1)
                t.transpose(pT[:, 64:64 + B], maskf[:], k.identf[0:B, 0:B]).then_inc(s_any, 1)
                t.wait_ge(s_trc, 1)
                t.matmul(pA[:, 0:B], k.ones[:], maskT[:], start=True, stop=True).then_inc(s_any, 1)

            @block.vector
            def _(v):
                link = Chain(v, s_dv)
                v.wait_ge(s_small, 16 * NSMALL)
                v.wait_ge(s_init, 1)
                v.tensor_scalar(maskf[:], maskr[:], 0, None, ALU.not_equal).then_inc(s_tr, 1)
                absmax = lambda o, i: v.tensor_reduce(out=o, in_=i, axis=AX_X, op=ALU.max, apply_absolute_value=True)
                for n, i in ((1, k.Wq[:]), (2, k.Wk[:]), (3, bqk[:, 0:1]), (4, bqk[:, 1:2]), (8, k.rWf[:])):
                    absmax(mx[:, n:n + 1], i)
                absmax(mx[0:NE * NC, 6:7], b1r[:])
                for n in range(4):
                    v.wait_ge(s_c[n], 16)
                    absmax(tmp6[:, n:n + 1], C[:, 8 * n:8 * n + 8, :].rearrange("p a b -> p (a b)"))
                link(v.memset(tmp6[:, 4:6], 0.0))
                link(absmax(mx[:, 0:1], tmp6[:]))
                for n in range(4):
                    v.wait_ge(s_x[n], 16)
                    for i in range(8 * n, 8 * n + 8):
                        v.bn_stats(st[:, i, :], k.X[:, i, :])
                link(v.memset(tmpn[:], 0.0))
                for i in range(NT):
                    v.bn_aggr(k.mv[:, i, :], st[:, i, :])
                link(v.memset(tmpn[:], 0.0))
                v.wait_ge(s_w1, 16 * NE)
                absmax(mx[:, 5:6], stage1[:])
                v.wait_ge(s_w2, 16 * NE)
                absmax(mx[:, 7:8], stage2[:]).then_inc(s_mx, 1)
                link(v.tensor_scalar(tmpv[:], k.mv[:, :, 1], EPS, None, ALU.add))
                rsqrt(v, link, k.rstd[:], tmpv[:], tmpn[:], NT)
                link(v.scalar_tensor_tensor(out=k.nmr[:], in0=k.mv[:, :, 0], scalar=-1.0, in1=k.rstd[:],
                                            op0=ALU.mult, op1=ALU.mult))
                v.wait_ge(s_mxa, 1)
                link(v.scalar_tensor_tensor(out=bound[:, 0:1], in0=mxa[:, 1:2], scalar=XN_NORM2, in1=mxa[:, 3:4], op0=ALU.mult, op1=ALU.add))
                link(v.tensor_tensor(tmp6[:, 0:1], mxa[:, 0:1], mxa[:, 2:3], ALU.mult))
                link(v.scalar_tensor_tensor(out=bound[:, 1:2], in0=tmp6[:, 0:1], scalar=float(D), in1=mxa[:, 4:5], op0=ALU.mult, op1=ALU.add))
                v.scalar_tensor_tensor(out=bound[:, 2:3], in0=mxa[:, 5:6], scalar=XN_NORM2, in1=mxa[:, 6:7], op0=ALU.mult, op1=ALU.add)
                v.tensor_copy(bound[:, 3:4], mxa[:, 5:6])
                link(v.tensor_copy(bound[:, 4:6], mxa[:, 7:9]))
                link(v.tensor_scalar(bound[:], bound[:], float(2.0 ** -60), float(2.0 ** 60), ALU.max, ALU.min))
                link(v.tensor_scalar(tmp6[:].bitcast(I32), bound[:].bitcast(I32), 0x7F800000, None, ALU.bitwise_and))
                v.tensor_scalar(k.sc[:, 0:2].bitcast(I32), tmp6[:, 0:2].bitcast(I32), -1.0, float(266 << 23), ALU.mult, ALU.add)
                link(v.tensor_scalar(k.sc[:, 2:6].bitcast(I32), tmp6[:, 2:6].bitcast(I32), -1.0, float(268 << 23), ALU.mult, ALU.add))
                link(v.tensor_scalar(k.inv[:].bitcast(I32), k.sc[:].bitcast(I32), -1.0, float(254 << 23), ALU.mult, ALU.add))
                v.memset(tmp6[:], 0.0).then_inc(s_scale, 1)
                v.tensor_tensor(k.bqk[:], bqk[:], k.sc[:, 0:2], ALU.mult)
                v.tensor_tensor(k.down[:, 0:1], k.inv[:, 2:3], k.inv[:, 4:5], ALU.mult)
                link(v.tensor_tensor(anyb[:, 0:1], k.inv[:, 0:1], k.inv[:, 1:2], ALU.mult))
                v.tensor_scalar(k.down[:, 1:2], k.down[:, 0:1], 1.0 / NS, None, ALU.mult)
                link(v.tensor_scalar(tmp6[:, 0:1], anyb[:, 0:1], float(HD ** -0.5), None, ALU.mult))
                v.tensor_tensor(k.b2s[:], k.b2[:, E * D:(E + 1) * D], k.b2[:, (E + 1) * D:NE * D], ALU.add)
                v.wait_ge(s_any, 1)
                v.tensor_copy(k.b1T[:], pT[:, 0:NE * NC])
                v.tensor_copy(maskT[:], pT[:, 64:64 + B]).then_inc(s_trc, 1)
                v.wait_ge(s_any, 2)
                link(v.tensor_scalar(anyb[:], pA[:, 0:B], 1.0, None, ALU.min))
                v.tensor_scalar(k.scl[:], anyb[:], tmp6[:, 0:1], None, ALU.mult)
                link(v.tensor_scalar(maskT[:], maskT[:], -1.0, 1e30, ALU.add, ALU.mult))
                v.tensor_tensor(k.mbias[:], maskT[:], anyb[:], ALU.mult)
                v.tensor_scalar(k.b2s[:], k.b2s[:], 1.0 / NS, None, ALU.mult)
                v.wait_ge(s_mask, 16)
                v.tensor_scalar(k.kmask[:], maski[:], 0, -BIG16, ALU.is_equal, ALU.mult)
                link(v.tensor_scalar(k.rW[:, 0:E], k.rWf[:], k.sc[:, 5:6], None, ALU.mult))
                v.scalar_tensor_tensor(out=k.rW[:, E:2 * E], in0=k.rWf[:], scalar=k.sc[:, 5:6], in1=k.rW[:, 0:E], op0=ALU.mult, op1=ALU.subtract)
                for n, (lo, hi, stg, sc) in enumerate(((k.W1l, k.W1h, stage1, 3), (k.W2l, k.W2h, stage2, 4))):
                    v.wait_ge(s_whi, n + 1)
                    v.scalar_tensor_tensor(out=lo[:], in0=stg[:], scalar=k.sc[:, sc:sc + 1], in1=hi[:], op0=ALU.mult, op1=ALU.subtract)


def attention(nc, io, k):
    with ExitStack() as ctx:
        sb = lambda n, s, d=F32: ctx.enter_context(nc.sbuf_tensor(n, s, d))
        sem = lambda n: ctx.enter_context(nc.semaphore(n))
        ps = lambda n, s, d=F32: ctx.enter_context(nc.psum_tensor(n, s, d))
        XN = sb("XN", [P, 2, D])
        CX = [sb(f"CX{u}", [P, 2, D]) for u in range(NB)]
        XCT = sb("XCT", [P, 4, P])
        QK32 = sb("QK32", [P, 2, W2T])
        QKS = [sb(f"QKS{u}", [P, 2, 2, W2T], F16) for u in range(NB)]
        PT = sb("PT", [P, 2, H, S])
        MX = sb("MX", [P, 2, 2, HD])
        NM = sb("NM", [P, 2, 2, HD])
        MP = sb("MP", [P, 2, 2, 2, HD], F16)
        MPT = [sb(f"MPT{u}", [4 * HD, 2, S], F16) for u in range(NB)]
        REC = sb("REC", [P, 2, S])
        AT = sb("AT", [P, 2, S])
        OT = sb("OT", [P, 2, D])
        ST6 = sb("ST6", [P, 2, 6])
        MV = sb("MV", [P, 2, 2])
        pT, pQK, pPV, pO = ps("pT2", [P, 4, P]), ps("pQK", [P, 2, W2T]), ps("pPV", [P, 2, 2, S]), ps("pO", [P, 512])
        pS = [ps(f"pS{n}", [P, 4, S]) for n in range(2)]
        pE = [ps(f"pE{n}", [P, 4, S]) for n in range(2)]
        names = "xn T XT qk hi lo ST S max mp nmT t2 exp pv cp op x1 vp vev dv z passed_act passed_pool passed_dve passed_sp"
        s = Parts(**{n: sem("a_" + n) for n in names.split()})
        s.c = [sem(f"a_c{u}") for u in range(NB)]
        s.w = [sem(f"a_w{u}") for u in range(NB)]
        s.rd = [sem(f"a_rd{u}") for u in range(NB)]
        s.m = [sem(f"a_m{u}") for u in range(NB)]
        N_W, N_RD, N_M = 16 * 5, 16 * 3, 16
        G = 8
        head = lambda g, j: 4 * j + g % 4

        def run(eng, body):
            for i in range(2 * NB):
                body(i, i % NB, True, i >= 1, i >= 2, i >= 3, i // NB)
            with eng.Fori(2, (NP - 1) // NB) as t:
                for u in range(NB):
                    body(NB * t + u, u, True, True, True, True, t)
            for i in range((NP - 1) // NB * NB, NP + 3):
                body(i, i % NB, i < NP, i <= NP, i <= NP + 1, True, i // NB)

        def earlier(n, u, t):
            return (u - n) % NB, t if u >= n else t - 1

        def pT16(tile):
            return tile[0:4 * HD, 0:1, :].rearrange("p a b -> p (a b)").bitcast(F16)

        with nc.Block() as block:
            @block.sync
            def _(sp):
                def load_context(i, v):
                    sp.dma_start(CX[v][:], io.ctx.rearrange("b s d -> s b d")[:, bass.ds(2 * i, 2), :]).then_inc(s.c[v], 16)

                load_context(0, 0)

                def body(i, u, a, b, c, o, t):
                    if a and not (isinstance(i, int) and i == NP - 1):
                        wait(sp, s.T, i - NB + 2)
                        load_context(i + 1, (u + 1) % NB)
                    if a:
                        qks = QKS[u]
                        wait(sp, s.lo, i + 1)
                        if not isinstance(i, int):
                            settle(sp, s.passed_sp)
                        wait(sp, s.rd[u], N_RD * t)
                        sp.dma_start(k.scrq[u][:, 0:2, :], qks[:, 0, :, :]).then_inc(s.w[u], 16)
                        sp.dma_start(k.scrq[u][:, 2, :], qks[:, 0, 0, :]).then_inc(s.w[u], 16)
                        sp.dma_start(k.scrk[u][:, 0, :], qks[:, 1, 0, :]).then_inc(s.w[u], 16)
                        sp.dma_start(k.scrk[u][:, 1:3, :], qks[:, 1, :, :]).then_inc(s.w[u], 16)
                        sp.dma_start(k.scrk[u][:, 3, :], k.kmask[:, bass.ds(i * W2T, W2T)]).then_inc(s.w[u], 16)
                    if a:
                        sp.wait_ge(s.w[u], N_W * t + N_W)
                        if not isinstance(i, int):
                            settle(sp, s.passed_sp)
                        wait(sp, s.ST, G * (i - 2))
                        sp.dma_start(k.Q[u][0:SHIFT, :, :], k.scrq[u].rearrange("(h2 pd) s t -> (pd s) h2 t", pd=2 * HD)).then_inc(s.rd[u], 16)
                        for par in range(2):
                            src = k.scrk[u].rearrange("(h2 par d) s t -> par (d s) h2 t", par=2, d=HD)[par]
                            sp.dma_start(k.K[u][SLOT_ROWS * par:SLOT_ROWS * (par + 1), par::2, :], src).then_inc(s.rd[u], 16)
                    if b:
                        v, tv = earlier(1, u, t)
                        sp.wait_ge(s.t2, i)
                        sp.dma_start(k.Q[v][SHIFT:SHIFT + 4, :, :], MPT[v][:].rearrange("p a b -> p (a b)")).then_inc(s.m[v], 16)
                run(sp, body)

            @block.gpsimd
            def _(g):
                def body(i, u, a, b, c, o, t):
                    if a and o:
                        g.wait_ge(s.ST, G * (i - 2))
                        if not isinstance(i, int):
                            settle(g, s.passed_pool)
                        g.memset(k.Q[u][SHIFT:SHIFT + 4, :, :], 0.0).then_inc(s.z, 1)
                run(g, body)

            @block.scalar
            def _(act):
                def normalise(i):
                    for bb in range(2):
                        ins = act.activation(XN[:, bb, :], k.X[:, bass.ds(2 * i + bb, 1), :].rearrange("p o d -> p (o d)"), ACT.Identity,
                                             bias=k.nmr[:, bass.ds(2 * i + bb, 1)], scale=k.rstd[:, bass.ds(2 * i + bb, 1)])
                    ins.then_inc(s.xn, 1)

                normalise(0)

                def body(i, u, a, b, c, o, t):
                    v, tv = earlier(1, u, t)
                    nxt = a and not (isinstance(i, int) and i == NP - 1)
                    if a:
                        act.wait_ge(s.T, i + 1)
                        act.activation(XCT[:], pT[:], ACT.Copy).then_inc(s.XT, 1)
                        act.wait_ge(s.qk, i + 1)
                        wait(act, s.lo, i)
                        wait(act, s.w[u], N_W * t)
                        for op in range(2):
                            bias, scale = k.bqk[:, op:op + 1], k.sc[:, op:op + 1]
                            act.activation(QK32[:, op, :], pQK[:, op, :], ACT.Identity, bias=bias, scale=scale)
                            ins = act.activation(QKS[u][:, op, 0, :], pQK[:, op, :], ACT.Identity, bias=bias, scale=scale)
                        ins.then_inc(s.hi, 1)
                    if c:
                        for g in range(G):
                            act.wait_ge(s.ST, G * (i - 2) + g + 1)
                            wait(act, s.pv, G * (i - 3) + g + 1)
                            if not isinstance(i, int):
                                settle(act, s.passed_act)
                            bt = 2 * (i - 2) + g // 4
                            act.activation(PT[:, g // 4, 4 * (g % 4):4 * (g % 4) + 4, :], pE[g % 2][:], ACT.Exp,
                                           bias=k.mbias[:, bass.ds(bt, 1)], scale=k.scl[:, bass.ds(bt, 1)]).then_inc(s.exp, 1)
                            if g == 5 and nxt:
                                normalise(i + 1)
                    if b:
                        act.wait_ge(s.nmT, i)
                        wait(act, s.m[v], N_M * tv)
                        act.activation(MPT[v][:].rearrange("p a b -> p (a b)"), pT16(pT), ACT.Copy).then_inc(s.t2, 1)
                    if nxt and not c:
                        normalise(i + 1)
                run(act, body)

            @block.tensor
            def _(pe):
                def scores(g, u, out, transposed):
                    for j in range(4):
                        h, q = head(g, j), S * (g // 4)
                        qo, ko = k.Q[u][:, h // 2, q:q + S], k.K[u][:, h, q:q + S]
                        ins = pe.matmul(out[:, j, :], ko if transposed else qo, qo if transposed else ko, start=True, stop=True)
                    return ins

                def body(i, u, a, b, c, o, t):
                    v, tv = earlier(1, u, t)
                    w, tw = earlier(2, u, t)
                    if a:
                        pe.wait_ge(s.xn, i + 1)
                        pe.wait_ge(s.c[u], 16 * t + 16)
                        wait(pe, s.t2, i - 1)
                        for bb in range(2):
                            pe.transpose(pT[:, bb, :], XN[:, bb, :], k.identf[:])
                        for bb in range(2):
                            ins = pe.transpose(pT[:, 2 + bb, :], CX[u][:, bb, :], k.identf[:])
                        ins.then_inc(s.T, 1)

                    def score(g):
                        if b and g < G:
                            if g == 0:
                                pe.wait_ge(s.rd[v], N_RD * tv + N_RD)
                                if not isinstance(i, int) or i > NB:
                                    pe.wait_ge(s.z, i - NB)
                            wait(pe, s.max, G * (i - 1) + g - 1)
                            scores(g, v, pS[g % 2], False).then_inc(s.S, 1)

                    score(0)
                    score(1)
                    if a:
                        pe.wait_ge(s.XT, i + 1)
                        wait(pe, s.vev, i)
                        pe.matmul(pQK[:, 0, :], k.Wq[:], XCT[:, 0:2, :].rearrange("p a b -> p (a b)"), start=True, stop=True)
                        pe.matmul(pQK[:, 1, :], k.Wk[:], XCT[:, 2:4, :].rearrange("p a b -> p (a b)"), start=True, stop=True).then_inc(s.qk, 1)
                    if o:
                        pe.wait_ge(s.cp, i - 2)
                        wait(pe, s.x1, i - 3)
                        for bb in range(2):
                            ins = pe.matmul(pO[:, D * bb:D * bb + D], AT[:, bb, :], k.Wo[:], start=True, stop=True)
                        ins.then_inc(s.op, 1)

                    def values(g):
                        m, bb = g % 4, g // 4
                        pe.wait_ge(s.exp, G * (i - 2) + g + 1)
                        if g == 0:
                            wait(pe, s.cp, i - 2)
                            pe.wait_ge(s.vev, i - 1)
                        for what in range(2):
                            for j in range(4):
                                lhs = k.V[w][:, 4 * bb + j, m, :] if what == 0 else k.onesV[:, m, :]
                                ins = pe.matmul(pPV[32 * j:32 * j + 32, bb, what, :], lhs, PT[:, bb, 4 * m + j, :],
                                                start=(g == 0 and what == 0), stop=(m == 3), skip_group_check=True)
                        ins.then_inc(s.pv, 1)

                    def project_values():
                        if a:
                            pe.wait_ge(s.hi, i + 1)
                            for bb in range(2):
                                ins = pe.matmul(pQK[:, 0, D * bb:D * bb + D], XCT[:, 2 + bb, :], k.Wv[:], start=True, stop=True)
                            ins.then_inc(s.vp, 1)

                    def transpose_shifts():
                        if b:
                            pe.wait_ge(s.mp, i)
                            wait(pe, s.XT, i + 1 if a else i)
                            for bb in range(2):
                                ins = pe.transpose(pT16(pT)[:, S * bb:S * bb + S], MP[:, bb].rearrange("p a b c -> p (a b c)"), k.ident16[:])
                            ins.then_inc(s.nmT, 1)

                    for g in range(G):
                        if g == 3:
                            project_values()
                        if c:
                            if g == 0:
                                pe.wait_ge(s.m[w], N_M * tw + N_M)
                            wait(pe, s.exp, G * (i - 2) + g - 1)
                            scores(g, w, pE[g % 2], True).then_inc(s.ST, 1)
                        score(g + 2)
                        if c and g:
                            values(g - 1)
                    transpose_shifts()
                    if c:
                        values(G - 1)
                run(pe, body)

            @block.vector
            def _(v_):
                link = Chain(v_, s.dv)

                def body(i, u, a, b, c, o, t):
                    v, tv = earlier(1, u, t)
                    w, tw = earlier(2, u, t)
                    link.restart()
                    def maxima(g):
                        if b:
                            v_.wait_ge(s.S, G * (i - 1) + g + 1)
                            m = g % 4
                            v_.tensor_reduce(out=MX[:, g // 4, m % 2, m // 2::2], in_=pS[g % 2][:], axis=AX_X, op=ALU.max).then_inc(s.max, 1)

                    def residual():
                        if o:
                            pair = k.X[:, bass.ds(2 * (i - 3), 2), :]
                            v_.wait_ge(s.op, i - 2)
                            link(v_.tensor_tensor(OT[:], pO[:, 0:2 * D].rearrange("p (a b) -> p a b", a=2), view(k.bo, 0, [0, 2], [1, D]), ALU.add))
                            v_.scalar_tensor_tensor(out=pair, in0=OT[:], scalar=k.gt[:, 0:1], in1=pair, op0=ALU.mult, op1=ALU.add).then_inc(s.x1, 1)
                            v_.wait_ge(s.x1, i - 2)
                            if not isinstance(i, int):
                                settle(v_, s.passed_dve)
                            for bb in range(2):
                                v_.bn_stats(ST6[:, bb, :], k.X[:, bass.ds(2 * (i - 3) + bb, 1), :].rearrange("p o d -> p (o d)"))
                            link(v_.memset(OT[:, 0, 0:2], 0.0))
                            for bb in range(2):
                                ins = v_.bn_aggr(MV[:, bb, :], ST6[:, bb, :])
                            link(ins)
                            v_.tensor_copy(k.mv[:, bass.ds(2 * (i - 3), 2), :], MV[:])

                    maxima(0)
                    maxima(1)
                    if a:
                        v_.wait_ge(s.hi, i + 1)
                        v_.tensor_tensor(QKS[u][:, :, 1, :], QK32[:], QKS[u][:, :, 0, :], ALU.subtract).then_inc(s.lo, 1)
                    maxima(2)
                    residual()
                    maxima(3)
                    maxima(4)
                    if a:
                        v_.wait_ge(s.vp, i + 1)
                        for bb in range(2):
                            ins = v_.tensor_tensor(view(k.V[u], 4 * bb * 4 * 32, [4 * 32, 4], [32 + HD, 4], [1, HD]),
                                                   pQK[:, 0, D * bb:D * bb + D].rearrange("p (j m d) -> p j m d", j=4, m=4),
                                                   k.bv[:].rearrange("p (j m d) -> p j m d", j=4, m=4), ALU.add)
                        ins.then_inc(s.vev, 1)
                    for g in range(5, G):
                        maxima(g)
                    if b:
                        v_.wait_ge(s.max, G * i)
                        link(v_.tensor_scalar(NM[:], MX[:], -SCORE_TOP, -1.0 / BIG16, ALU.max, ALU.mult))
                        wait(v_, s.nmT, i - 1)
                        link(v_.tensor_copy(MP[:, :, :, 0, :], NM[:]))
                        v_.tensor_tensor(MP[:, :, :, 1, :], NM[:], MP[:, :, :, 0, :], ALU.subtract).then_inc(s.mp, 1)
                    if c:
                        v_.wait_ge(s.pv, G * (i - 1))
                        link(v_.reciprocal(REC[:], pPV[:, :, 1, :]))
                        wait(v_, s.op, i - 2)
                        v_.tensor_tensor(AT[:], pPV[:, :, 0, :], REC[:], ALU.mult).then_inc(s.cp, 1)
                run(v_, body)


def normalise_and_gate(nc, io, k):
    with ExitStack() as ctx:
        sb = lambda n, s, d=F32: ctx.enter_context(nc.sbuf_tensor(n, s, d))
        sem = lambda n: ctx.enter_context(nc.semaphore(n))
        ps = lambda n, s, d=F32: ctx.enter_context(nc.psum_tensor(n, s, d))
        Q = 4
        XF = sb("XF", [P, Q, D])
        tmpn, tmpv = sb("tmpn2", [P, NT]), sb("tmpv2", [P, NT])
        pT = [ps(f"pTn{u}", [P, 2, Q, P], F16) for u in range(2)]
        pG = ps("pG", [P, NT, E])
        s_dv, s_pay, s_T, s_XT, s_gate, s_idx = (sem("g_" + n) for n in ("dv", "pay", "T", "XT", "gate", "idx"))

        def payload16(n, part):
            return k.PAY[:, bass.ds(n, Q), part * D // 2:(part + 1) * D // 2].bitcast(F16)

        with nc.Block() as block:
            @block.gpsimd
            def _(g):
                g.iota(k.PAY[:, :, D:ROW].rearrange("p n o -> p (n o)"), pattern=[[P, NT]], base=0, channel_multiplier=1)
                g.iota(k.em8[:], pattern=[[1, E]], base=-E, channel_multiplier=0, allow_small_or_imprecise_dtypes=True)
                g.iota(k.tiles[:], pattern=[[1, NTILE]], base=0, channel_multiplier=0, allow_small_or_imprecise_dtypes=True).then_inc(s_idx, 1)
                g.wait_ge(s_idx, 1)

            @block.vector
            def _(v):
                link = Chain(v, s_dv)
                link(v.tensor_scalar(tmpv[:], k.mv[:, :, 1], EPS, None, ALU.add))
                rsqrt(v, link, k.rstd[:], tmpv[:], tmpn[:], NT)
                link(v.scalar_tensor_tensor(out=k.nmr[:], in0=k.mv[:, :, 0], scalar=-1.0, in1=k.rstd[:],
                                            op0=ALU.mult, op1=ALU.mult))
                with v.Fori(0, NT // Q) as i:
                    link.restart()
                    for q in range(Q):
                        ins = v.tensor_scalar(XF[:, q, :], k.X[:, bass.ds(Q * i + q, 1), :].rearrange("p o d -> p (o d)"),
                                              k.rstd[:, bass.ds(Q * i + q, 1)], k.nmr[:, bass.ds(Q * i + q, 1)], ALU.mult, ALU.add)
                    link(ins)
                    link(v.tensor_copy(payload16(Q * i, 0), XF[:]))
                    v.tensor_tensor(payload16(Q * i, 1), XF[:], payload16(Q * i, 0), ALU.subtract).then_inc(s_pay, 1)
                    v.wait_ge(s_pay, i + 1)
                v.wait_ge(s_gate, NT // Q)
                link(v.tensor_scalar(k.G[:], pG[:], k.inv[:, 5:6], None, ALU.mult))
                link(v.tensor_tensor(k.G[:], k.G[:], view(k.rb, 0, [0, NT], [1, E]), ALU.add))

            @block.tensor
            def _(pe):
                def transposes(i, u, first):
                    pe.wait_ge(s_pay, i + 1)
                    if not first:
                        pe.wait_ge(s_XT, i - 1)
                    for part in range(2):
                        for q in range(Q):
                            ins = pe.transpose(pT[u][:, part, q, :], payload16(Q * i, part)[:, q, :], k.ident16[:])
                    ins.then_inc(s_T, 1)

                def gates(i):
                    pe.wait_ge(s_XT, i + 1)
                    for q in range(Q):
                        out = pG[:, bass.ds(Q * i + q, 1), :].rearrange("p o e -> p (o e)")
                        for step, (part, wpart) in enumerate(((0, 0), (1, 0), (0, 1))):
                            ins = pe.matmul(out, k.XT[:, part, bass.ds((Q * i + q) * P, P)], k.rW[:, E * wpart:E * wpart + E],
                                            start=(step == 0), stop=(step == 2))
                    ins.then_inc(s_gate, 1)

                transposes(0, 0, True)
                transposes(1, 1, True)
                gates(0)
                with pe.Fori(1, NT // Q // 2) as t:
                    for u in range(2):
                        transposes(2 * t + u, u, False)
                        gates(2 * t + u - 1)
                gates(NT // Q - 1)

            @block.scalar
            def _(a):
                with a.Fori(0, NT // Q // 2) as t:
                    for u in range(2):
                        i = 2 * t + u
                        a.wait_ge(s_T, i + 1)
                        a.activation(k.XT[:, :, bass.ds(i * Q * P, Q * P)], pT[u][:].rearrange("p a q t -> p a (q t)"), ACT.Copy).then_inc(s_XT, 1)


def route(nc, io, k):
    with ExitStack() as ctx:
        sb = lambda n, s, d=F32: ctx.enter_context(nc.sbuf_tensor(n, s, d))
        sem = lambda n: ctx.enter_context(nc.semaphore(n))
        ps = lambda n, s, d=F32: ctx.enter_context(nc.psum_tensor(n, s, d))
        O1, O2, tmp, G2 = (sb(n, [P, NT, E]) for n in ("O1", "O2", "tmpr", "G2"))
        Cb = sb("Cb", [P, NT, E], BF16)
        m1, m2, ix, ex = (sb(n, [P, NT]) for n in ("m1", "m2", "ix", "ex"))
        cnt, endf, startf = (sb(n, [P, E]) for n in ("cnt", "endf", "startf"))
        cnti = sb("cnti", [P, E], I32)
        ge = sb("ge", [P, NTILE, E - 1])
        pR, pC = ps("pR", [P, NT, E]), ps("pC", [P, NT, E])
        s_dv, s_c, s_cnt, s_ex, s_d = (sem("r_" + n) for n in ("dv", "c", "cnt", "ex", "d"))
        over_e = lambda t: view(t, 0, [1, NT], [0, E])
        over_n = lambda t: view(t, 0, [0, NT], [1, E])

        with nc.Block() as block:
            @block.vector
            def _(v):
                link = Chain(v, s_dv)
                for gates, top, one in ((k.G, m1, O1), (G2, m2, O2)):
                    link(v.tensor_reduce(out=top[:], in_=gates[:], axis=AX_X, op=ALU.max))
                    link(v.tensor_tensor(tmp[:], gates[:], over_e(top), ALU.is_equal))
                    link(v.tensor_tensor(tmp[:], tmp[:], over_n(k.em8), ALU.mult))
                    link(v.tensor_reduce(out=ix[:], in_=tmp[:], axis=AX_X, op=ALU.min))
                    link(v.tensor_tensor(one[:], over_n(k.em8), over_e(ix), ALU.is_equal))
                    if one is O1:
                        link(v.scalar_tensor_tensor(out=G2[:], in0=O1[:], scalar=-3e38, in1=k.G[:], op0=ALU.mult, op1=ALU.add))
                v.tensor_tensor(Cb[:], O1[:], O2[:], ALU.add).then_inc(s_c, 1)
                v.tensor_tensor(ix[:], m2[:], m1[:], ALU.subtract).then_inc(s_d, 1)
                v.wait_ge(s_cnt, 1)
                link(v.tensor_reduce(out=cnt[:], in_=pC[:].rearrange("p n e -> p e n"), axis=AX_X, op=ALU.add))
                link(v.tensor_scalar(cnt[:], cnt[:], float(TILE - 1), None, ALU.add))
                link(v.tensor_copy(cnti[:], cnt[:]))
                link(v.tensor_scalar(cnti[:], cnti[:], TILE.bit_length() - 1, None, ALU.arith_shift_right))
                link(v.tensor_copy(cnt[:], cnti[:]))
                link(v.tensor_copy(endf[:], cnt[:]))
                for e in range(1, E):
                    link(v.tensor_tensor(endf[:, e:e + 1], endf[:, e - 1:e], cnt[:, e:e + 1], ALU.add))
                link(v.tensor_tensor(startf[:], endf[:], cnt[:], ALU.subtract))
                link(v.tensor_scalar(startf[:], startf[:], float(TILE), None, ALU.mult))
                link(v.tensor_tensor(G2[:], pR[:], over_n(startf), ALU.add))
                for one, pos in ((O1, k.pos1), (O2, k.pos2)):
                    link(v.tensor_tensor(tmp[:], one[:], G2[:], ALU.mult))
                    link(v.tensor_reduce(out=m1[:], in_=tmp[:], axis=AX_X, op=ALU.add))
                    link(v.tensor_copy(pos[:], m1[:]))
                link(v.tensor_tensor(ge[:], view(k.tiles, 0, [1, NTILE], [0, E - 1]), view(endf, 0, [0, NTILE], [1, E - 1]), ALU.is_ge))
                link(v.tensor_reduce(out=k.tilef[:], in_=ge[:], axis=AX_X, op=ALU.add))
                link(v.tensor_copy(k.tilee[:], k.tilef[:]))
                v.wait_ge(s_ex, 1)
                link(v.tensor_scalar(m2[:], ex[:], 1.0, None, ALU.add))
                link(v.reciprocal(m1[:], m2[:]))
                link(v.tensor_scalar(k.w1[:], m1[:], k.gt[:, 1:2], None, ALU.mult))
                link(v.tensor_tensor(k.w2[:], k.w1[:], ex[:], ALU.mult))

            @block.scalar
            def _(a):
                a.wait_ge(s_d, 1)
                a.activation(ex[:], ix[:], ACT.Exp).then_inc(s_ex, 1)

            @block.tensor
            def _(pe):
                pe.wait_ge(s_c, 1)
                pe.matmul(pR[:].rearrange("p n e -> p (n e)"), k.lower[:], Cb[:].rearrange("p n e -> p (n e)"), start=True, stop=False, skip_group_check=True)
                for n in range(NT - 1):
                    pe.matmul(pR[:, n + 1:NT, :], k.onesb[:], view(Cb, n * E, [0, NT - 1 - n], [1, E]),
                              start=False, stop=(n == NT - 2), skip_group_check=True)
                pe.matmul(pC[:].rearrange("p n e -> p (n e)"), k.onesb[:], Cb[:].rearrange("p n e -> p (n e)"), start=True, stop=True).then_inc(s_cnt, 1)


def shared_experts(nc, io, k):
    with ExitStack() as ctx:
        sb = lambda n, s, d=F32: ctx.enter_context(nc.sbuf_tensor(n, s, d))
        sem = lambda n: ctx.enter_context(nc.semaphore(n))
        ps = lambda n, s, d=F32: ctx.enter_context(nc.psum_tensor(n, s, d))
        GT = 4 * P
        NGR = T // GT
        H32 = sb("H32", [P, NC, GT])
        HH = [sb(f"HH{u}", [P, 2, NC, GT], F16) for u in range(2)]
        OT = sb("OTs", [P, 4, D])
        pU = [ps(f"pU{c}", [P, GT]) for c in range(NC)]
        pD = [ps(f"pD{u}", [P, 4, D]) for u in range(2)]
        s = Parts(**{n: sem("s_" + n) for n in "up gelu hi lo dn x dv di io".split()})
        assert NS == 2

        with nc.Block() as block:
            @block.gpsimd
            def _(g):
                for choice, pos in enumerate((k.pos1, k.pos2)):
                    if choice:
                        g.wait_ge(s.di, 16 * NT)
                        g.iota(k.PAY[:, :, D:ROW].rearrange("p n o -> p (n o)"), pattern=[[P, NT]], base=T, channel_multiplier=1).then_inc(s.io, 1)
                        g.wait_ge(s.io, 1)
                    for n in range(NT):
                        g.indirect_dma_start(k.xs, bass.IndirectOffsetOnAxis(ap=pos[:, n:n + 1], axis=0), k.PAY[:, n, :], None).then_inc(s.di, 16)
                g.wait_ge(s.di, 2 * 16 * NT)

            def units(eng, body):
                for a in range(4):
                    body(0, a)
                with eng.Fori(1, NGR // 2 - 1) as t:
                    for a in range(4):
                        body(t, a)
                for a in range(4):
                    body(NGR // 2 - 1, a)

            @block.tensor
            def _(pe):
                def up(t, a):
                    i, e = 4 * t + a, a % 2
                    tok = bass.ds((2 * t + a // 2) * GT, GT)
                    for c in range(NC):
                        wait(pe, s.gelu, NC * (i - 1) + c + 1)
                        w0 = (E + e) * HID + c * P
                        for step, (w, part) in enumerate(((k.W1h, 0), (k.W1l, 0), (k.W1h, 1))):
                            ins = pe.matmul(pU[c][:], w[:, w0:w0 + P], k.XT[:, part, tok], start=(step == 0), stop=(step == 2))
                        ins.then_inc(s.up, 1)

                def down(t, a):
                    i, e, u = 4 * t + a, a % 2, a // 2
                    if e == 0:
                        wait(pe, s.x, 2 * t + u - 1)
                    for c in range(NC):
                        pe.wait_ge(s.lo, NC * i + c + 1)
                        w0 = (E + e) * HID + c * P
                        for q in range(4):
                            for step, (w, part) in enumerate(((k.W2h, 0), (k.W2l, 0), (k.W2h, 1))):
                                first = e == 0 and c == 0 and q == 0 and step == 0
                                ins = pe.matmul(pD[u][:, q, :], HH[e][:, part, c, q * P:(q + 1) * P], w[:, w0:w0 + P],
                                                start=first, stop=(e == 1 and c == NC - 1 and step == 2), skip_group_check=True)
                    ins.then_inc(s.dn, 1)

                def body(t, a):
                    if a < 3:
                        up(t, a + 1)
                    elif not (isinstance(t, int) and t == NGR // 2 - 1):
                        up(t + 1, 0)
                    down(t, a)

                up(0, 0)
                units(pe, body)

            @block.scalar
            def _(act):
                def body(t, a):
                    i, e = 4 * t + a, a % 2
                    for c in range(NC):
                        act.wait_ge(s.up, NC * i + c + 1)
                        wait(act, s.lo, NC * (i - 1) + c + 1)
                        col = (E + e) * NC + c
                        act.activation(H32[:, c, :], pU[c][:], ACT.Gelu, bias=k.b1T[:, col:col + 1], scale=k.inv[:, 3:4]).then_inc(s.gelu, 1)
                units(act, body)

            @block.vector
            def _(v):
                link = Chain(v, s.dv)
                def body(t, a):
                    i, e, u = 4 * t + a, a % 2, a // 2
                    for c in range(NC):
                        v.wait_ge(s.gelu, NC * i + c + 1)
                        if c == 0:
                            wait(v, s.dn, i - 1)
                        v.tensor_scalar(HH[e][:, 0, c, :], H32[:, c, :], k.sc[:, 2:3], None, ALU.mult).then_inc(s.hi, 1)
                        v.wait_ge(s.hi, NC * i + c + 1)
                        v.scalar_tensor_tensor(out=HH[e][:, 1, c, :], in0=H32[:, c, :], scalar=k.sc[:, 2:3], in1=HH[e][:, 0, c, :],
                                               op0=ALU.mult, op1=ALU.subtract).then_inc(s.lo, 1)
                    if a == 0:
                        finish(t - 1, 1) if not (isinstance(t, int) and t == 0) else None
                    elif a == 2:
                        finish(t, 0)

                def finish(t, u):
                    link.restart()
                    v.wait_ge(s.dn, 4 * t + 2 * u + 2)
                    link(v.scalar_tensor_tensor(out=OT[:], in0=pD[u][:], scalar=k.down[:, 1:2], in1=view(k.b2s, 0, [0, 4], [1, D]),
                                                op0=ALU.mult, op1=ALU.add))
                    rows = k.X[:, bass.ds(4 * (2 * t + u), 4), :]
                    v.scalar_tensor_tensor(out=rows, in0=OT[:], scalar=k.gt[:, 1:2], in1=rows, op0=ALU.mult, op1=ALU.add).then_inc(s.x, 1)
                    v.wait_ge(s.x, 2 * t + u + 1)
                units(v, body)
                finish(NGR // 2 - 1, 1)


def routed_experts(nc, io, k):
    with ExitStack() as ctx:
        sb = lambda n, s, d=F32: ctx.enter_context(nc.sbuf_tensor(n, s, d))
        sem = lambda n: ctx.enter_context(nc.semaphore(n))
        ps = lambda n, s, d=F32: ctx.enter_context(nc.psum_tensor(n, s, d))
        N = 6
        M = N // 2
        XR = [sb(f"XR{u}", [P, 2, ROW], I32) for u in range(N)]
        XE = [sb(f"XE{u}", [P, 2, TILE], F16) for u in range(M)]
        G32 = sb("G32", [P, NC, TILE])
        HR = [sb(f"HR{u}", [P, 2, NC, TILE], F16) for u in range(M)]
        Y = [sb(f"Y{u}", [P, 2, D]) for u in range(N)]
        pU = [ps(f"pUr{c}", [P, TILE]) for c in range(NC)]
        pD = [ps(f"pDr{u}", [P, 2, D]) for u in range(2)]
        pX = ps("pX", [P, 2, TILE], F16)
        s = Parts(**{n: sem("x_" + n) for n in "T XE up gelu hi lo dn y passed_sp passed_pool".split()})
        s.ld = [sem(f"x_ld{u}") for u in range(N)]
        s.st = [sem(f"x_st{u}") for u in range(N)]

        def tiles(eng, body, experts=False):
            def steps(i, t, count):
                es = load_experts(eng, i, min(count + 1, NTILE - i) if isinstance(i, int) else count + 1) if experts else []
                for u in range(count):
                    body(i + u, u, t, es[u:u + 2])

            full = (NTILE - 2) // N
            steps(0, 0, N)
            with eng.Fori(1, full) as t:
                steps(N * t, t, N)
            steps(N * full, full, NTILE - N * full)

        def load_experts(eng, i, count):
            _, values = nc.values_load_multi_w_load_instructions(
                k.tilee[0:1, bass.ds(i, count)], engines=[eng.engine], min_val=0, max_val=E - 1,
                skip_runtime_bounds_check_because="a sum of E - 1 comparisons")
            return values

        def more(i, n):
            return not isinstance(i, int) or i + n < NTILE

        with nc.Block() as block:
            @block.sync
            def _(sp):
                def body(i, u, t, es):
                    wait(sp, s.st[u], 32 * t)
                    if not isinstance(i, int):
                        settle(sp, s.passed_sp)
                    sp.dma_start(XR[u][:], k.xs[bass.ds(i * TILE, TILE), :].rearrange("(q p) w -> p q w", p=P)).then_inc(s.ld[u], 16)
                tiles(sp, body)

            @block.gpsimd
            def _(g):
                def body(i, u, t, es):
                    g.wait_ge(s.y, i + 1)
                    if not isinstance(i, int):
                        settle(g, s.passed_pool)
                    for q in range(2):
                        g.indirect_dma_start(k.yd, bass.IndirectOffsetOnAxis(ap=XR[u][:, q, D:ROW], axis=0), Y[u][:, q, :], None,
                                             bounds_check=2 * T - 1, oob_is_err=False).then_inc(s.st[u], 16)
                tiles(g, body)
                for u in range(N):
                    g.wait_ge(s.st[u], 32 * len(range(u, NTILE, N)))

            @block.tensor
            def _(pe):
                def transposes(i, u, t):
                    pe.wait_ge(s.ld[u], 16 * t + 16)
                    wait(pe, s.XE, i)
                    for part in range(2):
                        for q in range(2):
                            ins = pe.transpose(pX[:, part, q * P:(q + 1) * P], XR[u][:, q, part * D // 2:(part + 1) * D // 2].bitcast(F16), k.ident16[:])
                    ins.then_inc(s.T, 1)

                def up(i, u, e):
                    pe.wait_ge(s.XE, i + 1)
                    for c in range(NC):
                        wait(pe, s.gelu, NC * (i - 1) + c + 1)
                        for step, (w, part) in enumerate(((k.W1h, 0), (k.W1l, 0), (k.W1h, 1))):
                            ins = pe.matmul(pU[c][:], w[:, bass.ds(e * HID + c * P, P)], XE[u % M][:, part, :], start=(step == 0), stop=(step == 2))
                        ins.then_inc(s.up, 1)

                def down(i, u, e):
                    wait(pe, s.y, i - 1)
                    for c in range(NC):
                        if c % 2 == 0:
                            pe.wait_ge(s.lo, NC // 2 * i + c // 2 + 1)
                        for q in range(2):
                            for step, (w, part) in enumerate(((k.W2h, 0), (k.W2l, 0), (k.W2h, 1))):
                                ins = pe.matmul(pD[u % 2][:, q, :], HR[u % M][:, part, c, q * P:(q + 1) * P], w[:, bass.ds(e * HID + c * P, P)],
                                                start=(c == 0 and q == 0 and step == 0), stop=(c == NC - 1 and step == 2), skip_group_check=True)
                    ins.then_inc(s.dn, 1)

                def body(i, u, t, es):
                    if more(i, 2):
                        v, tv = ((u + 2) % N, t + (u + 2) // N)
                        transposes(i + 2, v, tv)
                    if more(i, 1):
                        up(i + 1, (u + 1) % N, es[1])
                    down(i, u, es[0])

                transposes(0, 0, 0)
                transposes(1, 1, 0)
                up(0, 0, load_experts(pe, 0, 1)[0])
                tiles(pe, body, experts=True)

            @block.scalar
            def _(act):
                def copy(i, u):
                    act.wait_ge(s.T, i + 1)
                    wait(act, s.up, NC * (i - M + 1))
                    act.activation(XE[u % M][:], pX[:], ACT.Copy).then_inc(s.XE, 1)

                def gelu(i, e):
                    for c in range(NC):
                        act.wait_ge(s.up, NC * i + c + 1)
                        wait(act, s.lo, NC // 2 * (i - 1) + c // 2 + 1)
                        act.activation(G32[:, c, :], pU[c][:], ACT.Gelu, bias=k.b1T[:, bass.ds(e * NC + c, 1)], scale=k.inv[:, 3:4]).then_inc(s.gelu, 1)

                def body(i, u, t, es):
                    if more(i, 2):
                        copy(i + 2, (u + 2) % N)
                    if more(i, 1):
                        gelu(i + 1, es[1])

                copy(0, 0)
                copy(1, 1)
                gelu(0, load_experts(act, 0, 1)[0])
                tiles(act, body, experts=True)

            @block.vector
            def _(v):
                def split(i, u):
                    for half in range(2):
                        ch = slice(2 * half, 2 * half + 2)
                        v.wait_ge(s.gelu, NC * i + 2 * half + 2)
                        wait(v, s.dn, i - M + 1)
                        v.tensor_scalar(HR[u % M][:, 0, ch, :], G32[:, ch, :], k.sc[:, 2:3], None, ALU.mult).then_inc(s.hi, 1)
                        v.wait_ge(s.hi, 2 * i + half + 1)
                        v.scalar_tensor_tensor(out=HR[u % M][:, 1, ch, :], in0=G32[:, ch, :], scalar=k.sc[:, 2:3], in1=HR[u % M][:, 0, ch, :],
                                               op0=ALU.mult, op1=ALU.subtract).then_inc(s.lo, 1)

                def result(i, u, t, e):
                    v.wait_ge(s.dn, i + 1)
                    wait(v, s.st[u], 32 * t)
                    for q in range(2):
                        ins = v.scalar_tensor_tensor(out=Y[u][:, q, :], in0=pD[u % 2][:, q, :], scalar=k.down[:, 0:1],
                                                     in1=k.b2[:, bass.ds(e * D, D)], op0=ALU.mult, op1=ALU.add)
                    ins.then_inc(s.y, 1)

                def body(i, u, t, es):
                    if more(i, 1):
                        split(i + 1, (u + 1) % N)
                    result(i, u, t, es[0])

                split(0, 0)
                tiles(v, body, experts=True)


def combine(nc, io, k):
    with ExitStack() as ctx:
        sb = lambda n, s, d=F32: ctx.enter_context(nc.sbuf_tensor(n, s, d))
        sem = lambda n: ctx.enter_context(nc.semaphore(n))
        NQ = 8
        R = NT // NQ
        YY = sb("YY", [P, 2, NT, D])
        s_ld = [sem(f"f_ld{n}") for n in range(NQ)]
        s_1, s_2, s_out = sem("f_1"), sem("f_2"), sem("f_out")
        yv = k.yd.rearrange("(c n p) d -> p c n d", c=2, p=P)
        with nc.Block() as block:
            @block.sync
            def _(sp):
                for n in range(NQ):
                    for c in range(2):
                        sp.dma_start(YY[:, c, R * n:R * n + R, :], yv[:, c, R * n:R * n + R, :]).then_inc(s_ld[n], 16)
                for n in range(NQ):
                    sp.wait_ge(s_2, n + 1)
                    sp.dma_start(io.out.rearrange("b s d -> s b d")[:, R * n:R * n + R, :], k.X[:, R * n:R * n + R, :]).then_inc(s_out, 16)
                sp.wait_ge(s_out, 16 * NQ)

            @block.vector
            def _(v):
                for n in range(NQ):
                    v.wait_ge(s_ld[n], 32)
                    for c, w, done in ((0, k.w1, s_1), (1, k.w2, s_2)):
                        for j in range(R * n, R * n + R):
                            ins = v.scalar_tensor_tensor(out=k.X[:, j, :], in0=YY[:, c, j, :], scalar=w[:, j:j + 1], in1=k.X[:, j, :],
                                                         op0=ALU.mult, op1=ALU.add)
                        ins.then_inc(done, 1)
                        if c == 0:
                            v.wait_ge(s_1, n + 1)


INPUTS = {"x": "x", "ctx_1024": "ctx", "mask_BxS2_if1": "mask", "g_xattn": "g1", "g_ffn": "g2",
          "L0_xattn_Wq": "Wq", "L0_xattn_bq": "bq", "L0_xattn_Wk": "Wk", "L0_xattn_bk": "bk",
          "L0_xattn_Wv": "Wv", "L0_xattn_bv": "bv", "L0_xattn_Wo": "Wo", "L0_xattn_bo": "bo",
          "L0_ffn_rW": "rW", "L0_ffn_rb": "rb", "L0_ffn_W1": "W1", "L0_ffn_b1": "b1", "L0_ffn_W2": "W2", "L0_ffn_b2": "b2",
          "L0_ffn_sW1": "sW1", "L0_ffn_sb1": "sb1", "L0_ffn_sW2": "sW2", "L0_ffn_sb2": "sb2"}


def program(nc, stages=9, **io):
    io = Parts(**io)
    dram = lambda n, s, d: nc.dram_tensor(n, s, d, kind="Internal").ap()
    with ExitStack() as outer:
        def alloc(ctx, k, **tiles):
            for n, (shape, dt) in tiles.items():
                k[n] = ctx.enter_context(nc.sbuf_tensor("t_" + n, shape, dt))
        k = Parts()
        alloc(outer, k, X=([P, NT, D], F32), W1h=([P, NE * HID], F16), W1l=([P, NE * HID], F16),
              W2h=([P, NE * HID], F16), W2l=([P, NE * HID], F16),
              identf=([P, P], F32), ident16=([P, P], F16), ones=([P, P], F32), onesb=([P, P], BF16), lower=([P, P], BF16),
              b2=([P, NE * D], F32), b2s=([P, D], F32), b1T=([P, NE * NC], F32), gt=([P, 2], F32), rb=([P, E], F32),
              rW=([P, 2 * E], F16), sc=([P, 6], F32), inv=([P, 6], F32), down=([P, 2], F32), mv=([P, NT, 2], F32),
              rstd=([P, NT], F32), nmr=([P, NT], F32))
        k.xs = dram("xs", (SLOTS, ROW), I32)
        k.yd = dram("yd", (2 * T, D), F32)
        k.scrq = [dram(f"scrq{u}", (P, 4, W2T), F16) for u in range(NB)]
        k.scrk = [dram(f"scrk{u}", (P, 4, W2T), F16) for u in range(NB)]
        with ExitStack() as a:
            alloc(a, k, Wq=([P, P], F32), Wk=([P, P], F32), Wv=([P, P], F32), Wo=([P, P], F32),
                  bv=([P, D], F32), bo=([P, D], F32), rWf=([P, E], F32), bqk=([P, 2], F32),
                  onesV=([P, 4, 4 * HD], F32), scl=([P, B], F32), mbias=([P, B], F32), kmask=([P, T], F16))
            k.update(Q=[], K=[], V=[])
            for u in range(NB):
                alloc(a, k, **{f"Q{u}": ([P, HD, W2T], F16), f"K{u}": ([P, H, W2T], F16), f"V{u}": ([P, 8, 4, 32], F32)})
                for n in "QKV":
                    k[n].append(k[f"{n}{u}"])
            prologue(nc, io, k)
            attention(nc, io, k)
        with ExitStack() as b:
            alloc(b, k, XT=([P, 2, T], F16), w1=([P, NT], F32), w2=([P, NT], F32), tilef=([P, NTILE], F32), tilee=([P, NTILE], I32))
            with ExitStack() as c:
                alloc(c, k, PAY=([P, NT, ROW], I32), G=([P, NT, E], F32), em8=([P, E], F32), tiles=([P, NTILE], F32),
                      pos1=([P, NT], I32), pos2=([P, NT], I32))
                normalise_and_gate(nc, io, k)
                route(nc, io, k)
                shared_experts(nc, io, k)
            routed_experts(nc, io, k)
            combine(nc, io, k)


def kernel(**inputs):
    import numpy as np
    import concourse.bacc as bacc
    from concourse.bass_utils import run_bass_kernel_spmd

    nc = bacc.Bacc("TRN2", target_bir_lowering=False, num_devices=1)
    arrays, io = {}, {}
    for name, short in INPUTS.items():
        a = np.ascontiguousarray(inputs[name])
        arrays["in_" + short] = a
        io[short] = nc.dram_tensor("in_" + short, a.shape, mybir.dt.from_np(a.dtype), kind="ExternalInput").ap()
    io["out"] = nc.dram_tensor("out", (B, S, D), F32, kind="ExternalOutput").ap()
    program(nc, **io)
    return run_bass_kernel_spmd(nc, [arrays], core_ids=[0]).results[0]["out"]
```

```python
import concourse.bass as bass
from concourse import mybir
from contextlib import ExitStack

F32 = mybir.dt.float32
F16 = mybir.dt.float16
BF16 = mybir.dt.bfloat16
I32 = mybir.dt.int32
ALU = mybir.AluOpType
ACT = mybir.ActivationFunctionType
AX_X = mybir.AxisListType.X

P = 128
B, S, D = 32, 128, 128
T = B * S
NT = T // P
H, HD = 16, 8
NP = B // 2
W2T = 2 * S
E, NS = 8, 2
NE = E + NS
HID = 512
NC = HID // P
TILE = 256
NTILE = (2 * T + E * (TILE - 1)) // TILE
SLOTS = NTILE * TILE
XS_ROWS = -(-SLOTS // (P * NE)) * P * NE
ROW = D + 1
NOWHERE = 1 << 20
EPS = 1e-5
XN_NORM2 = 128.2
RSQRT_SEED = 0x5F3759DF
SLOT_ROWS = 4 * HD
SHIFT = 2 * SLOT_ROWS
NB = 3
BIG16 = 32768.0
BIG16_TWICE = 2.0 ** 113 * (1 + 0x7800 / 2 ** 23)
SCORE_TOP = float(2 ** 29)


class Parts(dict):

    def __getattr__(self, name):
        return self[name]


def view(tile, off, *dims, parts=P, p0=0):
    full = tile[:]
    step = full.ap[0][0]
    return bass.AP(tensor=full.tensor, offset=full.offset + p0 * step + off, ap=[[step, parts], *[list(d) for d in dims]])


def wait(eng, sem, value):
    if not isinstance(value, int) or value > 0:
        eng.wait_ge(sem, value)


def settle(eng, passed):
    eng.sem_inc(passed, 1)


class Chain:

    def __init__(self, eng, sem):
        self.eng, self.sem, self.n = eng, sem, 0

    def __call__(self, ins):
        self.n += 1
        ins.then_inc(self.sem, 1)
        self.eng.wait_ge(self.sem, self.n)

    def restart(self):
        self.eng.sem_clear(self.sem)
        self.n = 0


def rsqrt(v, link, out, x, tmp, n):
    link(v.tensor_scalar(tmp.bitcast(I32), x.bitcast(I32), 1, None, ALU.arith_shift_right))
    link(v.tensor_scalar(out.bitcast(I32), tmp.bitcast(I32), -1.0, float(RSQRT_SEED), ALU.mult, ALU.add))
    for _ in range(3):
        link(v.scalar_tensor_tensor(out=tmp, in0=out, scalar=-0.5, in1=out, op0=ALU.mult, op1=ALU.mult))
        link(v.tensor_tensor(tmp, tmp, x, ALU.mult))
        link(v.scalar_tensor_tensor(out=out, in0=tmp, scalar=1.5, in1=out, op0=ALU.add, op1=ALU.mult))


def prologue(nc, io, k):
    with ExitStack() as ctx:
        sb = lambda n, s, d=F32: ctx.enter_context(nc.sbuf_tensor(n, s, d))
        sem = lambda n: ctx.enter_context(nc.semaphore(n))
        ps = lambda n, s, d=F32: ctx.enter_context(nc.psum_tensor(n, s, d))
        C = sb("C", [P, NT, D])
        maskr = sb("maskr", [B, S], I32)
        maskf = sb("maskf", [B, S])
        kmrow = sb("kmrow", [B, S], F16)
        mx = sb("mx", [P, 9])
        mxa = sb("mxa", [P, 5])
        st = sb("st", [P, NT, 6])
        tmpn, tmpv = sb("tmpn", [P, NT]), sb("tmpv", [P, NT])
        tmp2 = sb("tmp2", [P, 2])
        maskT = sb("maskT", [P, B])
        anyb = sb("anyb", [P, B])
        graw = sb("graw", [P, 2])
        bqk = sb("bqk", [P, 2])
        bvr = sb("bvr", [P, P])
        constq = sb("constq", [P, W2T], F16)
        pT, pA, pB = (ps(n, [P, 512]) for n in ("pT", "pA", "pB"))
        s_x = [sem(f"s_x{n}") for n in range(4)]
        s_c = [sem(f"s_c{n}") for n in range(4)]
        names = "first rest ident mx mxa tr trc any bvr q0 km pad padw init gl dv one st"
        s = Parts({n: sem("p_" + n) for n in names.split()})

        first = [(k.Wq[:], io.Wq), (k.Wk[:], io.Wk),
                 (bqk[:, 0:1], io.bq.rearrange("(p o) -> p o", o=1)), (bqk[:, 1:2], io.bk.rearrange("(p o) -> p o", o=1)),
                 (maskr[:], io.mask), (k.bvc[:], io.bv.rearrange("(p o) -> p o", o=1))]
        rest = [(k.Wv[:], io.Wv), (k.Wo[:], io.Wo), (k.bo[:], io.bo.partition_broadcast(P)),
                (graw[:, 0:1], io.g1.partition_broadcast(P)), (graw[:, 1:2], io.g2.partition_broadcast(P)),
                (k.b1r[0:E * NC, :], io.b1.rearrange("e (c p) -> (e c) p", p=P)),
                (k.b1r[E * NC:NE * NC, :], io.sb1.rearrange("e (c p) -> (e c) p", p=P)),
                (k.rWf[:], io.rW), (k.rb[:], io.rb.partition_broadcast(P)),
                (k.b2[:, 0:E * D], io.b2.rearrange("e d -> (e d)").partition_broadcast(P)),
                (k.b2[:, E * D:NE * D], io.sb2.rearrange("e d -> (e d)").partition_broadcast(P))]

        with nc.Block() as block:
            @block.sync
            def _(sp):
                xv = io.x.rearrange("b s d -> s b d")
                cv = io.ctx.rearrange("b s d -> s b d")
                for n in range(4):
                    sp.dma_start(C[:, 8 * n:8 * n + 8, :], cv[:, 8 * n:8 * n + 8, :]).then_inc(s_c[n], 16)
                    sp.dma_start(k.X[:, 8 * n:8 * n + 8, :], xv[:, 8 * n:8 * n + 8, :]).then_inc(s_x[n], 16)
                sp.dma_start(k.CX[0][:], cv[:, 0:2, :]).then_inc(k.s_c[0], 16)
                sp.wait_ge(s.first, 16 * len(first))
                w1 = k.stage1[:].rearrange("p (e h) -> p e h", h=HID)
                w2 = k.stage2[:].rearrange("p (e d) -> p e d", d=D)
                sp.dma_start(w1[:, 0:E, :], io.W1.rearrange("e d h -> d e h")).then_inc(k.s_w, 16)
                sp.dma_start(w1[:, E:NE, :], io.sW1.rearrange("e d h -> d e h")).then_inc(k.s_w, 16)
                sp.wait_ge(s.pad, 16 * NB)
                sp.dma_start(w2[:, 0:E * NC, :], io.W2.rearrange("e (c p) d -> p (e c) d", p=P)).then_inc(k.s_w, 16)
                sp.dma_start(w2[:, E * NC:NE * NC, :], io.sW2.rearrange("e (c p) d -> p (e c) d", p=P)).then_inc(k.s_w, 16)

            @block.gpsimd
            def _(g):
                g.memset(k.identf[:], 0.0)
                g.memset(k.ident16[:], 0.0)
                g.memset(k.ones[:], 1.0)
                g.memset(k.onesb[:], 1.0)
                g.memset(k.lower[:], 1.0)
                g.memset(constq[:], BIG16)
                g.memset(k.onesV[:], 0.0)
                g.memset(k.K[0][:].rearrange("p a b -> p (a b)").bitcast(F32), 0.0).then_inc(s.init, 1)
                g.wait_ge(s.init, 1)
                for m in (k.identf, k.ident16):
                    g.affine_select(out=m[:], in_=m[:], compare_op=ALU.not_equal, fill=1.0, base=0,
                                    pattern=[[-1, P]], channel_multiplier=1)
                g.affine_select(out=k.lower[:], in_=k.lower[:], compare_op=ALU.is_gt, fill=0.0, base=0,
                                pattern=[[1, P]], channel_multiplier=-1)
                for i in range(4):
                    last = g.memset(k.onesV[:, i, HD * i:HD * i + HD], 1.0)
                last.then_inc(s.ident, 1)
                for u in range(1, NB):
                    g.memset(k.K[u][:].rearrange("p a b -> p (a b)").bitcast(F32), 0.0)
                g.memset(k.padrow[:, 0:D], 0)
                g.memset(k.padrow[:, D:ROW], NOWHERE).then_inc(s.init, 1)
                g.wait_ge(s.init, 2)
                for u in range(NB):
                    for par in range(2):
                        row = SHIFT + 32 * par
                        ins = g.memset(k.K[u][row:row + 2, par::2, :].bitcast(F32), BIG16_TWICE)
                ins.then_inc(s.padw, 1)
                g.wait_ge(s.padw, 1)
                g.wait_ge(s.mx, 1)
                g.partition_all_reduce(mxa[:], mx[:, 0:5], P, bass.bass_isa.ReduceOp.max).then_inc(s.mxa, 1)

            @block.scalar
            def _(a):
                for dst, src in first:
                    a.dma_start(dst, src).then_inc(s.first, 16)
                for dst, src in rest:
                    a.dma_start(dst, src).then_inc(s.rest, 16)
                a.wait_ge(s.km, 1)
                a.dma_start(k.kmd.rearrange("(b s) -> b s", s=S), kmrow[:]).then_inc(s.one, 16)
                a.wait_ge(s.init, 1)
                for u in range(NB):
                    a.dma_start(k.scr[u][0, :, 3, :], constq[:]).then_inc(s.pad, 16)
                a.wait_ge(s.rest, 16 * len(rest))
                a.activation(k.gt[:], graw[:], ACT.Tanh).then_inc(s.gl, 1)
                a.wait_ge(s.gl, 1)
                a.wait_ge(s.one, 16)
                a.wait_ge(s.pad, 16 * NB)

            @block.tensor
            def _(t):
                t.wait_ge(s.ident, 1)
                t.wait_ge(s.tr, 1)
                t.transpose(pT[:, 64:64 + B], maskf[:], k.identf[0:B, 0:B]).then_inc(s.any, 1)
                t.wait_ge(s.trc, 1)
                t.matmul(pA[:, 0:B], k.ones[:], maskT[:], start=True, stop=True).then_inc(s.any, 1)
                t.wait_ge(s.rest, 16 * len(rest))
                t.transpose(pB[:, 256:256 + NE * NC], k.b1r[:], k.identf[0:NE * NC, 0:NE * NC])
                t.wait_ge(s.bvr, 1)
                t.matmul(pB[:, 0:D], bvr[:], k.Wo[:], start=True, stop=True).then_inc(s.any, 1)

            @block.vector
            def _(v):
                link = Chain(v, s.dv)
                zero = lambda t: v.memset(t[:].rearrange("p a b -> p (a b)").bitcast(F32), 0.0)
                for u in range(NB):
                    zero(k.Q[u])
                    v.memset(k.V[u][:].rearrange("p a b c -> p (a b c)"), 0.0)
                absmax = lambda o, i: v.tensor_reduce(out=o, in_=i, axis=AX_X, op=ALU.max, apply_absolute_value=True)
                for n in range(4):
                    v.wait_ge(s_c[n], 16)
                    absmax(mx[:, 5 + n:6 + n], C[:, 8 * n:8 * n + 8, :].rearrange("p a b -> p (a b)"))
                    v.wait_ge(s_x[n], 16)
                    for i in range(8 * n, 8 * n + 8):
                        ins = v.bn_stats(st[:, i, :], k.X[:, i, :])
                    ins.then_inc(s.st, 1)
                    if n == 0:
                        v.wait_ge(s.first, 16 * len(first))
                        v.tensor_scalar(kmrow[:], maskr[:], 0, -BIG16, ALU.is_equal, ALU.mult).then_inc(s.km, 1)
                    if n:
                        v.wait_ge(s.st, n)
                        for i in range(8 * n - 8, 8 * n):
                            v.bn_aggr(k.mv[:, i, :], st[:, i, :])
                for n, i in ((1, k.Wq[:]), (2, k.Wk[:]), (3, bqk[:, 0:1]), (4, bqk[:, 1:2])):
                    absmax(mx[:, n:n + 1], i)
                v.tensor_scalar(maskf[:], maskr[:], 0, None, ALU.not_equal).then_inc(s.tr, 1)
                link(v.memset(tmpn[:], 0.0))
                v.tensor_reduce(out=mx[:, 0:1], in_=mx[:, 5:9], axis=AX_X, op=ALU.max).then_inc(s.mx, 1)
                for i in range(NT - 8, NT):
                    v.bn_aggr(k.mv[:, i, :], st[:, i, :])
                link(v.memset(tmpn[:], 0.0))
                link(v.tensor_scalar(tmpv[:], k.mv[:, :, 1], EPS, None, ALU.add))
                rsqrt(v, link, k.rstd[:], tmpv[:], tmpn[:], NT)
                link(v.scalar_tensor_tensor(out=k.nmr[:], in0=k.mv[:, :, 0], scalar=-1.0, in1=k.rstd[:],
                                            op0=ALU.mult, op1=ALU.mult))
                v.wait_ge(s.mxa, 1)
                v.scalar_tensor_tensor(out=k.bound[:, 0:1], in0=mxa[:, 1:2], scalar=XN_NORM2, in1=mxa[:, 3:4], op0=ALU.mult, op1=ALU.add)
                link(v.tensor_tensor(tmp2[:, 0:1], mxa[:, 0:1], mxa[:, 2:3], ALU.mult))
                link(v.scalar_tensor_tensor(out=k.bound[:, 1:2], in0=tmp2[:, 0:1], scalar=float(D), in1=mxa[:, 4:5], op0=ALU.mult, op1=ALU.add))
                scales(v, link, k, 0, 2, 13)
                v.tensor_tensor(k.bqk[:], bqk[:], k.sc[:, 0:2], ALU.mult)
                link(v.tensor_tensor(anyb[:, 0:1], k.inv[:, 0:1], k.inv[:, 1:2], ALU.mult))
                link(v.tensor_scalar(tmp2[:, 0:1], anyb[:, 0:1], float(HD ** -0.5), None, ALU.mult))
                v.wait_ge(s.any, 1)
                v.tensor_copy(maskT[:], pT[:, 64:64 + B]).then_inc(s.trc, 1)
                v.tensor_scalar(bvr[:], k.ones[:], k.bvc[:], None, ALU.mult).then_inc(s.bvr, 1)
                v.wait_ge(s.any, 2)
                link(v.tensor_scalar(anyb[:], pA[:, 0:B], 1.0, None, ALU.min))
                v.tensor_scalar(k.scl[:], anyb[:], tmp2[:, 0:1], None, ALU.mult)
                link(v.tensor_scalar(maskT[:], maskT[:], -1.0, 1e30, ALU.add, ALU.mult))
                v.tensor_tensor(k.mbias[:], maskT[:], anyb[:], ALU.mult)
                v.wait_ge(s.any, 3)
                v.tensor_copy(k.b1T[:], pB[:, 256:256 + NE * NC])
                link(v.tensor_tensor(k.bo2[:], pB[:, 0:D], k.bo[:], ALU.add))
                v.wait_ge(s.gl, 1)
                v.tensor_scalar(k.gbo[:], k.bo2[:], k.gt[:, 0:1], None, ALU.mult)


def scales(v, link, k, a, b, top):
    link(v.tensor_scalar(k.bound[:, a:b], k.bound[:, a:b], float(2.0 ** -60), float(2.0 ** 60), ALU.max, ALU.min))
    link(v.tensor_scalar(k.pow2[:, a:b].bitcast(I32), k.bound[:, a:b].bitcast(I32), 0x7F800000, None, ALU.bitwise_and))
    link(v.tensor_scalar(k.sc[:, a:b].bitcast(I32), k.pow2[:, a:b].bitcast(I32), -1.0, float((253 + top) << 23), ALU.mult, ALU.add))
    link(v.tensor_scalar(k.inv[:, a:b].bitcast(I32), k.sc[:, a:b].bitcast(I32), -1.0, float(254 << 23), ALU.mult, ALU.add))


def attention(nc, io, k):
    with ExitStack() as ctx:
        sb = lambda n, s, d=F32: ctx.enter_context(nc.sbuf_tensor(n, s, d))
        sem = lambda n: ctx.enter_context(nc.semaphore(n))
        ps = lambda n, s, d=F32: ctx.enter_context(nc.psum_tensor(n, s, d))
        XN = sb("XN", [P, 2, D])
        CX = k.CX
        XCT = sb("XCT", [P, 4, P])
        QK32 = sb("QK32", [P, 2, W2T])
        QKS = [sb(f"QKS{u}", [P, 2, 2, W2T], F16) for u in range(NB)]
        PT = sb("PT", [P, 2, H, S])
        MX = sb("MX", [P, 2, 2, HD])
        NM = sb("NM", [P, 2, 2, HD])
        MP = sb("MP", [P, 2, 2, 2, HD], F16)
        MPT = [sb(f"MPT{u}", [4 * HD, 2, S], F16) for u in range(NB)]
        REC = sb("REC", [P, S])
        AT = [sb(f"AT{bb}", [P, S]) for bb in range(2)]
        OT = sb("OT", [P, 2])
        ST6 = sb("ST6", [P, 2, 6])
        MV = sb("MV", [P, 2, 2])
        mxw, mxwa = sb("mxw", [P, 4]), sb("mxwa", [P, 4])
        SPLIT = (NP - 1) // NB * NB - NE
        pT, pQK = ps("pT2", [P, 4, P]), ps("pQK", [P, 2, W2T])
        pA = [ps(f"pAtt{bb}", [P, 4, S]) for bb in range(2)]
        pS = [ps(f"pS{n}", [P, 4, S]) for n in range(2)]
        pE = [ps(f"pE{n}", [P, 4, S]) for n in range(2)]
        names = "xn T XT qk qk32 lo ST S max mp nmT t2 exp pv cp0 cp1 op0 op1 x0 x1 vp vev dv z bias wm wa ws wh passed_act passed_pool passed_dve passed_sp"
        s = Parts(**{n: sem("a_" + n) for n in names.split()})
        s.cp, s.op, s.x = (s.cp0, s.cp1), (s.op0, s.op1), (s.x0, s.x1)
        s.c = k.s_c
        s.w = [sem(f"a_w{u}") for u in range(NB)]
        s.rd = [sem(f"a_rd{u}") for u in range(NB)]
        s.m = [sem(f"a_m{u}") for u in range(NB)]
        N_W, N_RD, N_M = 16 * 3, 16 * 3, 16 * 2
        G = 8
        head = lambda g, j: 4 * j + g % 4

        def run(eng, body):
            for i in range(2 * NB):
                body(i, i % NB, True, i >= 1, i >= 2, i >= 3, i // NB)
            with eng.Fori(2, (NP - 1) // NB) as t:
                for u in range(NB):
                    body(NB * t + u, u, True, True, True, True, t)
            for i in range((NP - 1) // NB * NB, NP + 3):
                body(i, i % NB, i < NP, i <= NP, i <= NP + 1, True, i // NB)

        def earlier(n, u, t):
            return (u - n) % NB, t if u >= n else t - 1

        shifts16 = pQK[0:4 * HD, 0, 0:S].bitcast(F16)

        with nc.Block() as block:
            @block.sync
            def _(sp):
                def load_context(i, v):
                    sp.dma_start(CX[v][:], io.ctx.rearrange("b s d -> s b d")[:, bass.ds(2 * i, 2), :]).then_inc(s.c[v], 16)

                head_dim, operand = 4 * W2T, P * 4 * W2T

                def body(i, u, a, b, c, o, t):
                    if a and not (isinstance(i, int) and i == NP - 1):
                        wait(sp, s.T, i - 1)
                        if not isinstance(i, int):
                            settle(sp, s.passed_sp)
                        load_context(i + 1, (u + 1) % NB)
                    if a:
                        scr, qks = k.scr[u], QKS[u]
                        wait(sp, s.rd[u], N_RD * t)
                        if not isinstance(i, int):
                            settle(sp, s.passed_sp)
                        sp.dma_start(scr[1, :, 3, :], k.kmd[bass.ds(i * W2T, W2T)].partition_broadcast(P)).then_inc(s.w[u], 16)
                        wait(sp, s.lo, i + 1)
                        if not isinstance(i, int):
                            settle(sp, s.passed_sp)
                        sp.dma_start(bass.AP(tensor=scr.tensor, offset=scr.offset, ap=[[head_dim, P], [operand + W2T, 2], [1, 2 * W2T]]),
                                     qks[:].rearrange("p a b t -> p a (b t)")).then_inc(s.w[u], 16)
                        sp.dma_start(bass.AP(tensor=scr.tensor, offset=scr.offset + 2 * W2T, ap=[[head_dim, P], [operand - 2 * W2T, 2], [1, W2T]]),
                                     qks[:, :, 0, :]).then_inc(s.w[u], 16)
                        sp.wait_ge(s.w[u], N_W * t + N_W)
                        if not isinstance(i, int):
                            settle(sp, s.passed_sp)
                        wait(sp, s.ST, G * (i - 2))
                        sp.dma_start(k.Q[u][0:SHIFT, :, :], scr[0].rearrange("(h2 pd) s t -> (pd s) h2 t", pd=2 * HD)).then_inc(s.rd[u], 16)
                        for par in range(2):
                            src = scr[1].rearrange("(h2 par d) s t -> par (d s) h2 t", par=2, d=HD)[par]
                            sp.dma_start(k.K[u][SLOT_ROWS * par:SLOT_ROWS * (par + 1), par::2, :], src).then_inc(s.rd[u], 16)
                    if b:
                        v, tv = earlier(1, u, t)
                        sp.wait_ge(s.t2, i)
                        for par in range(2):
                            row = SHIFT + 32 * par
                            sp.dma_start(k.Q[v][row:row + 2, :, :], MPT[v][2 * HD * par:2 * HD * (par + 1)].rearrange("p a b -> p (a b)")).then_inc(s.m[v], 16)
                        if not isinstance(i, int) or i == SPLIT:
                            rows = XS_ROWS // NE
                            sp.dma_start(k.xs[bass.ds((i - SPLIT) * rows, rows), :].rearrange("(p r) w -> p r w", p=P),
                                         view(k.padrow, 0, [0, rows // P], [1, ROW])).then_inc(k.s_empty, 16)
                run(sp, body)

            @block.gpsimd
            def _(g):
                def body(i, u, a, b, c, o, t):
                    if a and o:
                        g.wait_ge(s.ST, G * (i - 2))
                        if not isinstance(i, int):
                            settle(g, s.passed_pool)
                        g.memset(k.Q[u][SHIFT:P, :, :], 0.0).then_inc(s.z, 1)
                        g.wait_ge(s.z, i - 2)
                    if a:
                        pair = k.X[:, bass.ds(2 * i, 2), :]
                        g.wait_ge(s.xn, i + 1)
                        if not isinstance(i, int):
                            settle(g, s.passed_pool)
                        g.tensor_tensor(pair, pair, view(k.gbo, 0, [0, 2], [1, D]), ALU.add).then_inc(s.bias, 1)
                        g.wait_ge(s.bias, i + 1)
                    if isinstance(i, int) and i == 1:
                        g.wait_ge(s.wm, 1)
                        g.partition_all_reduce(mxwa[:], mxw[:], P, bass.bass_isa.ReduceOp.max).then_inc(s.wa, 1)
                        g.wait_ge(s.wa, 1)
                run(g, body)

            @block.scalar
            def _(act):
                def normalise(i):
                    for bb in range(2):
                        ins = act.activation(XN[:, bb, :], k.X[:, bass.ds(2 * i + bb, 1), :].rearrange("p o d -> p (o d)"), ACT.Identity,
                                             bias=k.nmr[:, bass.ds(2 * i + bb, 1)], scale=k.rstd[:, bass.ds(2 * i + bb, 1)])
                    ins.then_inc(s.xn, 1)

                def transposed(i):
                    act.wait_ge(s.T, i + 1)
                    act.activation(XCT[:], pT[:], ACT.Copy).then_inc(s.XT, 1)

                normalise(0)
                transposed(0)

                def body(i, u, a, b, c, o, t):
                    v, tv = earlier(1, u, t)
                    nxt = a and not (isinstance(i, int) and i == NP - 1)
                    if a:
                        act.wait_ge(s.qk, i + 1)
                        wait(act, s.lo, i)
                        for op in range(2):
                            ins = act.activation(QK32[:, op, :], pQK[:, op, :], ACT.Identity, bias=k.bqk[:, op:op + 1], scale=k.sc[:, op:op + 1])
                        ins.then_inc(s.qk32, 1)
                    for g in range(G):
                        if g == 2 and a:
                            act.wait_ge(s.vp, i + 1)
                            for bb in range(2):
                                ins = act.activation(view(k.V[u], 4 * bb * 4 * 32, [4 * 32, 4], [32 + HD, 4], [1, HD]),
                                                     pQK[:, 0, D * bb:D * bb + D].rearrange("p (j m d) -> p j m d", j=4, m=4), ACT.Copy)
                            ins.then_inc(s.vev, 1)
                        if g == 6 and nxt:
                            transposed(i + 1)
                        if g == 6 and b:
                            act.wait_ge(s.nmT, i)
                            wait(act, s.m[v], N_M * tv)
                            act.activation(MPT[v][:].rearrange("p a b -> p (a b)"), shifts16, ACT.Copy).then_inc(s.t2, 1)
                        if c:
                            act.wait_ge(s.ST, G * (i - 2) + g + 1)
                            wait(act, s.pv, G * (i - 3) + g + 1)
                            if not isinstance(i, int):
                                settle(act, s.passed_act)
                            bt = 2 * (i - 2) + g // 4
                            act.activation(PT[:, g // 4, 4 * (g % 4):4 * (g % 4) + 4, :], pE[g % 2][:], ACT.Exp,
                                           bias=k.mbias[:, bass.ds(bt, 1)], scale=k.scl[:, bass.ds(bt, 1)]).then_inc(s.exp, 1)
                        if g == 1 and nxt:
                            normalise(i + 1)
                        if isinstance(i, int) and i == SPLIT and g == 0:
                            act.wait_ge(s.ws, 1)
                        if g in (0, 4) and (not isinstance(i, int) or i == SPLIT):
                            hi, stg, sc = ((k.W1h, k.stage1, 3), (k.W2h, k.stage2, 4))[g // 4]
                            cols = bass.ds((i - SPLIT) * HID, HID)
                            act.activation(hi[:, cols], stg[:, cols], ACT.Copy, scale=k.sc[:, sc:sc + 1]).then_inc(s.wh, 1)
                run(act, body)

            @block.tensor
            def _(pe):
                def scores(g, u, out, transposed):
                    for j in range(4):
                        h, q = head(g, j), S * (g // 4)
                        qo, ko = k.Q[u][:, h // 2, q:q + S], k.K[u][:, h, q:q + S]
                        ins = pe.matmul(out[:, j, :], ko if transposed else qo, qo if transposed else ko, start=True, stop=True)
                    return ins

                def transposes(i, u, t):
                    pe.wait_ge(s.xn, i + 1)
                    pe.wait_ge(s.c[u], 16 * t + 16)
                    for bb in range(2):
                        pe.transpose(pT[:, bb, :], XN[:, bb, :], k.identf[:])
                    for bb in range(2):
                        ins = pe.transpose(pT[:, 2 + bb, :], CX[u][:, bb, :], k.identf[:])
                    ins.then_inc(s.T, 1)

                def project_queries_keys(i):
                    pe.wait_ge(s.XT, i + 1)
                    wait(pe, s.vev, i)
                    wait(pe, s.t2, i - 1)
                    pe.matmul(pQK[:, 0, :], k.Wq[:], XCT[:, 0:2, :].rearrange("p a b -> p (a b)"), start=True, stop=True)
                    pe.matmul(pQK[:, 1, :], k.Wk[:], XCT[:, 2:4, :].rearrange("p a b -> p (a b)"), start=True, stop=True).then_inc(s.qk, 1)

                transposes(0, 0, 0)
                project_queries_keys(0)

                def body(i, u, a, b, c, o, t):
                    v, tv = earlier(1, u, t)
                    w, tw = earlier(2, u, t)
                    nxt = a and not (isinstance(i, int) and i == NP - 1)

                    def score(g):
                        if b and g < G:
                            if g == 0:
                                pe.wait_ge(s.rd[v], N_RD * tv + N_RD)
                                if not isinstance(i, int) or i > NB:
                                    pe.wait_ge(s.z, i - NB)
                            wait(pe, s.max, G * (i - 1) + g - 1)
                            scores(g, v, pS[g % 2], False).then_inc(s.S, 1)


                    def project_output(bb, pair):
                        pe.wait_ge(s.cp[bb], pair + 1)
                        pe.matmul(pA[bb][:, 2, :], AT[bb][:], k.Wo[:], start=True, stop=True, skip_group_check=True).then_inc(s.op[bb], 1)

                    def values(g):
                        m, bb = g % 4, g // 4
                        pe.wait_ge(s.exp, G * (i - 2) + g + 1)
                        if m == 0:
                            wait(pe, s.x[bb], i - 2)
                        if g == 0:
                            pe.wait_ge(s.vev, i - 1)
                        for what in range(2):
                            for j in range(4):
                                lhs = k.V[w][:, 4 * bb + j, m, :] if what == 0 else k.onesV[:, m, :]
                                ins = pe.matmul(pA[bb][32 * j:32 * j + 32, what, :], lhs, PT[:, bb, 4 * m + j, :],
                                                start=(m == 0 and what == 0), stop=(m == 3), skip_group_check=True)
                        ins.then_inc(s.pv, 1)

                    def project_values():
                        if a:
                            pe.wait_ge(s.qk32, i + 1)
                            for bb in range(2):
                                ins = pe.matmul(pQK[:, 0, D * bb:D * bb + D], XCT[:, 2 + bb, :], k.Wv[:], start=True, stop=True)
                            ins.then_inc(s.vp, 1)

                    def transpose_shifts():
                        if b:
                            pe.wait_ge(s.mp, i)
                            if a:
                                pe.wait_ge(s.vev, i + 1)
                            for bb in range(2):
                                ins = pe.transpose(shifts16[:, S * bb:S * bb + S], MP[:, bb].rearrange("p a b c -> p (a b c)"), k.ident16[:])
                            ins.then_inc(s.nmT, 1)

                    def shifted_scores(g):
                        if c and g < G:
                            if g == 0:
                                pe.wait_ge(s.m[w], N_M * tw + N_M)
                            wait(pe, s.exp, G * (i - 2) + g - 1)
                            scores(g, w, pE[g % 2], True).then_inc(s.ST, 1)

                    score(0)
                    score(1)
                    shifted_scores(0)
                    score(2)
                    shifted_scores(1)
                    score(3)
                    for g in range(G):
                        score(g + 4)
                        if g == 1:
                            project_values()
                        if g == 2 and o:
                            project_output(1, i - 3)
                        if g == 4 and nxt:
                            transposes(i + 1, (u + 1) % NB, t + (u + 1) // NB)
                        if g == 5:
                            transpose_shifts()
                        if g == 6 and c:
                            project_output(0, i - 2)
                        if g == 6 and nxt:
                            project_queries_keys(i + 1)
                        if c:
                            values(g)
                        shifted_scores(g + 2)
                run(pe, body)

            @block.vector
            def _(v_):
                link = Chain(v_, s.dv)
                absmax = lambda o, i: v_.tensor_reduce(out=o, in_=i, axis=AX_X, op=ALU.max, apply_absolute_value=True)

                def low_part(i, n):
                    if not isinstance(i, int) or i == SPLIT:
                        lo, hi, stg, sc = ((k.W1l, k.W1h, k.stage1, 3), (k.W2l, k.W2h, k.stage2, 4))[n]
                        cols = bass.ds((i - SPLIT) * HID, HID)
                        v_.wait_ge(s.wh, 2 * (i - SPLIT) + n + 1)
                        v_.scalar_tensor_tensor(out=lo[:, cols], in0=stg[:, cols], scalar=k.sc[:, sc:sc + 1], in1=hi[:, cols],
                                                op0=ALU.mult, op1=ALU.subtract)

                def weights(i):
                    if not isinstance(i, int):
                        return
                    if i == 0:
                        link(v_.memset(mxw[:], 0.0))
                        v_.wait_ge(k.s_w, 16 * 4)
                        absmax(mxw[:, 0:1], k.stage1[:])
                        absmax(mxw[0:NE * NC, 1:2], k.b1r[:])
                        v_.tensor_tensor(k.b2s[:], k.b2[:, E * D:(E + 1) * D], k.b2[:, (E + 1) * D:NE * D], ALU.add)
                    elif i == 1:
                        absmax(mxw[:, 3:4], k.rWf[:])
                        absmax(mxw[:, 2:3], k.stage2[:]).then_inc(s.wm, 1)
                        link(v_.tensor_scalar(k.b2s[:], k.b2s[:], 1.0 / NS, None, ALU.mult))
                    elif i == 2:
                        v_.wait_ge(s.wa, 1)
                        v_.scalar_tensor_tensor(out=k.bound[:, 2:3], in0=mxwa[:, 0:1], scalar=XN_NORM2, in1=mxwa[:, 1:2], op0=ALU.mult, op1=ALU.add)
                        v_.tensor_copy(k.bound[:, 3:4], mxwa[:, 0:1])
                        link(v_.tensor_copy(k.bound[:, 4:6], mxwa[:, 2:4]))
                        scales(v_, link, k, 2, 6, 15)
                        link(v_.tensor_tensor(k.down[:, 0:1], k.inv[:, 2:3], k.inv[:, 4:5], ALU.mult))
                        link(v_.tensor_scalar(k.down[:, 1:2], k.down[:, 0:1], 1.0 / NS, None, ALU.mult))
                        link(v_.tensor_scalar(k.rW[:, 0:E], k.rWf[:], k.sc[:, 5:6], None, ALU.mult))
                        v_.scalar_tensor_tensor(out=k.rW[:, E:2 * E], in0=k.rWf[:], scalar=k.sc[:, 5:6], in1=k.rW[:, 0:E],
                                                op0=ALU.mult, op1=ALU.subtract).then_inc(s.ws, 1)

                def body(i, u, a, b, c, o, t):
                    v, tv = earlier(1, u, t)
                    w, tw = earlier(2, u, t)
                    link.restart()
                    def maxima(g):
                        if b:
                            v_.wait_ge(s.S, G * (i - 1) + g + 1)
                            m = g % 4
                            v_.tensor_reduce(out=MX[:, g // 4, m % 2, m // 2::2], in_=pS[g % 2][:], axis=AX_X, op=ALU.max).then_inc(s.max, 1)

                    def normalised(bb, pair):
                        v_.wait_ge(s.pv, G * pair + 4 * bb + 4)
                        link(v_.reciprocal(REC[:], pA[bb][:, 1, :]))
                        wait(v_, s.op[bb], pair)
                        v_.tensor_tensor(AT[bb][:], pA[bb][:, 0, :], REC[:], ALU.mult).then_inc(s.cp[bb], 1)

                    def residual(bb, pair):
                        row = k.X[:, bass.ds(2 * pair + bb, 1), :].rearrange("p o d -> p (o d)")
                        v_.wait_ge(s.op[bb], pair + 1)
                        v_.wait_ge(s.bias, pair + 1)
                        v_.scalar_tensor_tensor(out=row, in0=pA[bb][:, 2, :], scalar=k.gt[:, 0:1], in1=row, op0=ALU.mult, op1=ALU.add).then_inc(s.x[bb], 1)

                    def statistics(bb, pair):
                        v_.wait_ge(s.x[bb], pair + 1)
                        if not isinstance(i, int):
                            settle(v_, s.passed_dve)
                        v_.bn_stats(ST6[:, bb, :], k.X[:, bass.ds(2 * pair + bb, 1), :].rearrange("p o d -> p (o d)"))

                    maxima(0)
                    maxima(1)
                    maxima(2)
                    maxima(3)
                    if a:
                        v_.wait_ge(s.qk32, i + 1)
                        wait(v_, s.w[u], N_W * t)
                        link(v_.tensor_copy(QKS[u][:, :, 0, :], QK32[:]))
                        v_.tensor_tensor(QKS[u][:, :, 1, :], QK32[:], QKS[u][:, :, 0, :], ALU.subtract).then_inc(s.lo, 1)
                    if o:
                        normalised(1, i - 3)
                    maxima(4)
                    maxima(5)
                    if o:
                        residual(1, i - 3)
                    maxima(6)
                    maxima(7)
                    if b:
                        v_.wait_ge(s.max, G * i)
                        link(v_.tensor_scalar(NM[:], MX[:], -SCORE_TOP, -1.0 / BIG16, ALU.max, ALU.mult))
                        wait(v_, s.nmT, i - 1)
                        link(v_.tensor_copy(MP[:, :, :, 0, :], NM[:]))
                        v_.tensor_tensor(MP[:, :, :, 1, :], NM[:], MP[:, :, :, 0, :], ALU.subtract).then_inc(s.mp, 1)
                    if c:
                        normalised(0, i - 2)
                    low_part(i, 0)
                    low_part(i, 1)
                    if c:
                        residual(0, i - 2)
                    if o:
                        statistics(1, i - 3)
                    if c:
                        statistics(0, i - 2)
                    if o or c:
                        link(v_.memset(OT[:], 0.0))
                        for bb, pair in ([(1, i - 3)] if o else []) + ([(0, i - 2)] if c else []):
                            ins = v_.bn_aggr(MV[:, 1 - bb, :], ST6[:, bb, :])
                        link(ins)
                        for bb, pair in ([(1, i - 3)] if o else []) + ([(0, i - 2)] if c else []):
                            v_.tensor_copy(k.mv[:, bass.ds(2 * pair + bb, 1), :].rearrange("p o d -> p (o d)"), MV[:, 1 - bb, :])
                    weights(i)
                run(v_, body)


def normalise_and_gate(nc, io, k):
    with ExitStack() as ctx:
        sb = lambda n, s, d=F32: ctx.enter_context(nc.sbuf_tensor(n, s, d))
        sem = lambda n: ctx.enter_context(nc.semaphore(n))
        ps = lambda n, s, d=F32: ctx.enter_context(nc.psum_tensor(n, s, d))
        Q = 4
        XF = [sb(f"XF{u}", [P, Q, D]) for u in range(2)]
        tmpn, tmpv = sb("tmpn2", [P, NT]), sb("tmpv2", [P, NT])
        pT = [ps(f"pTn{u}", [P, 2, Q, P], F16) for u in range(2)]
        pG = ps("pG", [P, NT, E])
        s_dv, s_pay, s_T, s_XT, s_gate, s_idx = (sem("g_" + n) for n in ("dv", "pay", "T", "XT", "gate", "idx"))
        s_ln, s_xn, s_hi, s_passed = sem("g_ln"), sem("g_xn"), sem("g_hi"), sem("g_passed")

        def payload16(n, part):
            return k.PAY[:, bass.ds(n, Q), part * D // 2:(part + 1) * D // 2].bitcast(F16)

        with nc.Block() as block:
            @block.gpsimd
            def _(g):
                g.iota(k.PAY[:, :, D:ROW].rearrange("p n o -> p (n o)"), pattern=[[P, NT]], base=0, channel_multiplier=1)
                g.iota(k.em8[:], pattern=[[1, E]], base=-E, channel_multiplier=0, allow_small_or_imprecise_dtypes=True)
                g.iota(k.tiles[:], pattern=[[1, NTILE]], base=0, channel_multiplier=0, allow_small_or_imprecise_dtypes=True).then_inc(s_idx, 1)
                g.wait_ge(s_idx, 1)

            @block.vector
            def _(v):
                link = Chain(v, s_dv)
                link(v.tensor_scalar(tmpv[:], k.mv[:, :, 1], EPS, None, ALU.add))
                rsqrt(v, link, k.rstd[:], tmpv[:], tmpn[:], NT)
                link(v.scalar_tensor_tensor(out=k.nmr[:], in0=k.mv[:, :, 0], scalar=-1.0, in1=k.rstd[:],
                                            op0=ALU.mult, op1=ALU.mult))
                v.memset(tmpn[:, 0:1], 0.0).then_inc(s_ln, 1)

                def split(i, u):
                    v.wait_ge(s_xn, i + 1)
                    v.tensor_copy(payload16(Q * i, 0), XF[u][:]).then_inc(s_hi, 1)
                    v.wait_ge(s_hi, i + 1)
                    v.tensor_tensor(payload16(Q * i, 1), XF[u][:], payload16(Q * i, 0), ALU.subtract).then_inc(s_pay, 1)

                def copy_transposed(i, u):
                    v.wait_ge(s_T, i + 1)
                    v.tensor_copy(k.XT[:, :, bass.ds(i * Q * P, Q * P)], pT[u][:].rearrange("p a q t -> p a (q t)")).then_inc(s_XT, 1)

                split(0, 0)
                split(1, 1)
                with v.Fori(0, NT // Q // 2 - 1) as t:
                    for u in range(2):
                        copy_transposed(2 * t + u, u)
                        split(2 * t + u + 2, u)
                for u in range(2):
                    copy_transposed(NT // Q - 2 + u, u)
                v.wait_ge(s_gate, NT // Q)
                link(v.tensor_scalar(k.G[:], pG[:], k.inv[:, 5:6], None, ALU.mult))
                link(v.tensor_tensor(k.G[:], k.G[:], view(k.rb, 0, [0, NT], [1, E]), ALU.add))

            @block.tensor
            def _(pe):
                def transposes(i, u, first):
                    pe.wait_ge(s_pay, i + 1)
                    if not first:
                        pe.wait_ge(s_XT, i - 1)
                    for part in range(2):
                        for q in range(Q):
                            ins = pe.transpose(pT[u][:, part, q, :], payload16(Q * i, part)[:, q, :], k.ident16[:])
                    ins.then_inc(s_T, 1)

                def gates(i):
                    pe.wait_ge(s_XT, i + 1)
                    for q in range(Q):
                        out = pG[:, bass.ds(Q * i + q, 1), :].rearrange("p o e -> p (o e)")
                        for step, (part, wpart) in enumerate(((0, 0), (1, 0), (0, 1))):
                            ins = pe.matmul(out, k.XT[:, part, bass.ds((Q * i + q) * P, P)], k.rW[:, E * wpart:E * wpart + E],
                                            start=(step == 0), stop=(step == 2))
                    ins.then_inc(s_gate, 1)

                transposes(0, 0, True)
                transposes(1, 1, True)
                gates(0)
                with pe.Fori(1, NT // Q // 2) as t:
                    for u in range(2):
                        transposes(2 * t + u, u, False)
                        gates(2 * t + u - 1)
                gates(NT // Q - 1)

            @block.scalar
            def _(a):
                a.wait_ge(s_ln, 1)

                def normalise(i, u):
                    for q in range(Q):
                        ins = a.activation(XF[u][:, q, :], k.X[:, bass.ds(Q * i + q, 1), :].rearrange("p o d -> p (o d)"), ACT.Identity,
                                           bias=k.nmr[:, bass.ds(Q * i + q, 1)], scale=k.rstd[:, bass.ds(Q * i + q, 1)])
                    ins.then_inc(s_xn, 1)

                normalise(0, 0)
                normalise(1, 1)
                with a.Fori(1, NT // Q // 2) as t:
                    for u in range(2):
                        a.wait_ge(s_pay, 2 * t + u - 1)
                        settle(a, s_passed)
                        normalise(2 * t + u, u)


def route_and_shared(nc, io, k):
    with ExitStack() as ctx:
        sb = lambda n, s, d=F32: ctx.enter_context(nc.sbuf_tensor(n, s, d))
        sem = lambda n: ctx.enter_context(nc.semaphore(n))
        ps = lambda n, s, d=F32: ctx.enter_context(nc.psum_tensor(n, s, d))
        GT = 4 * P
        NGR = T // GT
        H32 = sb("H32", [P, NC, GT])
        HH = [sb(f"HH{u}", [P, 2, NC, GT], F16) for u in range(2)]
        OT = sb("OTs", [P, 4, D])
        pU = [ps(f"pU{c}", [P, GT]) for c in range(NC)]
        pD = [ps(f"pD{u}", [P, 4, D]) for u in range(2)]
        s = Parts(**{n: sem("s_" + n) for n in "up gelu hi hia lo dn x dv di io choices counts differ exp slots".split()})
        O1, O2, tmp, G2 = (sb(n, [P, NT, E]) for n in ("O1", "O2", "tmpr", "G2"))
        Cb = sb("Cb", [P, NT, E], BF16)
        m1, m2, ix, ex = (sb(n, [P, NT]) for n in ("m1", "m2", "ix", "ex"))
        cntp = sb("cntp", [P, NT])
        cnt, endf, startf = (sb(n, [P, E]) for n in ("cnt", "endf", "startf"))
        cnti = sb("cnti", [P, E], I32)
        ge = sb("ge", [P, NTILE, E - 1])
        pR, pC = ps("pR", [P, NT, E]), ps("pC", [P, NT, E])
        over_e = lambda t: view(t, 0, [1, NT], [0, E])
        over_n = lambda t: view(t, 0, [0, NT], [1, E])
        assert NS == 2

        with nc.Block() as block:
            @block.gpsimd
            def _(g):
                g.wait_ge(k.s_empty, 16 * NE)
                g.wait_ge(s.slots, 1)
                for choice, pos in enumerate((k.pos1, k.pos2)):
                    if choice:
                        g.wait_ge(s.di, 16 * NT)
                        g.iota(k.PAY[:, :, D:ROW].rearrange("p n o -> p (n o)"), pattern=[[P, NT]], base=T, channel_multiplier=1).then_inc(s.io, 1)
                        g.wait_ge(s.io, 1)
                    for n in range(NT):
                        g.indirect_dma_start(k.xs, bass.IndirectOffsetOnAxis(ap=pos[:, n:n + 1], axis=0), k.PAY[:, n, :], None).then_inc(s.di, 16)
                g.wait_ge(s.di, 2 * 16 * NT)

            def units(eng, body):
                for a in range(4):
                    body(0, a)
                with eng.Fori(1, NGR // 2 - 1) as t:
                    for a in range(4):
                        body(t, a)
                for a in range(4):
                    body(NGR // 2 - 1, a)

            @block.tensor
            def _(pe):
                def up(t, a):
                    i, e = 4 * t + a, a % 2
                    tok = bass.ds((2 * t + a // 2) * GT, GT)
                    for c in range(NC):
                        wait(pe, s.gelu, NC * (i - 1) + c + 1)
                        w0 = (E + e) * HID + c * P
                        for step, (w, part) in enumerate(((k.W1h, 0), (k.W1l, 0), (k.W1h, 1))):
                            ins = pe.matmul(pU[c][:], w[:, w0:w0 + P], k.XT[:, part, tok], start=(step == 0), stop=(step == 2))
                        ins.then_inc(s.up, 1)

                def down(t, a):
                    i, e, u = 4 * t + a, a % 2, a // 2
                    if e == 0:
                        wait(pe, s.x, 2 * t + u - 1)
                    for c in range(NC):
                        pe.wait_ge(s.lo, NC * i + c + 1)
                        w0 = (E + e) * HID + c * P
                        for q in range(4):
                            for step, (w, part) in enumerate(((k.W2h, 0), (k.W2l, 0), (k.W2h, 1))):
                                first = e == 0 and c == 0 and q == 0 and step == 0
                                ins = pe.matmul(pD[u][:, q, :], HH[e][:, part, c, q * P:(q + 1) * P], w[:, w0:w0 + P],
                                                start=first, stop=(e == 1 and c == NC - 1 and step == 2), skip_group_check=True)
                    ins.then_inc(s.dn, 1)

                def prefixes():
                    pe.wait_ge(s.choices, 1)
                    flat = lambda t: t[:].rearrange("p n e -> p (n e)")
                    pe.matmul(flat(pR), k.lower[:], flat(Cb), start=True, stop=False, skip_group_check=True)
                    for n in range(NT - 1):
                        pe.matmul(pR[:, n + 1:NT, :], k.onesb[:], view(Cb, n * E, [0, NT - 1 - n], [1, E]),
                                  start=False, stop=(n == NT - 2), skip_group_check=True)
                    pe.matmul(flat(pC), k.onesb[:], flat(Cb), start=True, stop=True).then_inc(s.counts, 1)

                def body(t, a):
                    if a < 3:
                        up(t, a + 1)
                    elif not (isinstance(t, int) and t == NGR // 2 - 1):
                        up(t + 1, 0)
                    if isinstance(t, int) and t == 0 and a == 0:
                        prefixes()
                    down(t, a)

                up(0, 0)
                units(pe, body)

            @block.scalar
            def _(act):
                def body(t, a):
                    i, e = 4 * t + a, a % 2
                    for c in range(NC):
                        act.wait_ge(s.up, NC * i + c + 1)
                        wait(act, s.lo, NC * (i - 1) + c + 1)
                        col = (E + e) * NC + c
                        act.activation(H32[:, c, :], pU[c][:], ACT.Gelu, bias=k.b1T[:, col:col + 1], scale=k.inv[:, 3:4]).then_inc(s.gelu, 1)
                        if c % 2:
                            act.wait_ge(s.gelu, NC * i + c)
                            if c == 1:
                                wait(act, s.dn, i - 1)
                            act.activation(HH[e][:, 0, c - 1, :], H32[:, c - 1, :], ACT.Copy, scale=k.sc[:, 2:3]).then_inc(s.hia, 1)
                    if isinstance(t, int) and t == 0 and a == 0:
                        act.wait_ge(s.differ, 1)
                        act.activation(ex[:], ix[:], ACT.Exp).then_inc(s.exp, 1)
                units(act, body)

            @block.vector
            def _(v):
                link = Chain(v, s.dv)
                def body(t, a):
                    i, e, u = 4 * t + a, a % 2, a // 2
                    for c in range(NC):
                        if c == 0:
                            wait(v, s.dn, i - 1)
                        if c % 2:
                            v.wait_ge(s.gelu, NC * i + c + 1)
                            v.tensor_scalar(HH[e][:, 0, c, :], H32[:, c, :], k.sc[:, 2:3], None, ALU.mult).then_inc(s.hi, 1)
                            v.wait_ge(s.hi, 2 * i + c // 2 + 1)
                        else:
                            v.wait_ge(s.hia, 2 * i + c // 2 + 1)
                        v.scalar_tensor_tensor(out=HH[e][:, 1, c, :], in0=H32[:, c, :], scalar=k.sc[:, 2:3], in1=HH[e][:, 0, c, :],
                                               op0=ALU.mult, op1=ALU.subtract).then_inc(s.lo, 1)
                    if a == 0:
                        finish(t - 1, 1) if not (isinstance(t, int) and t == 0) else None
                    elif a == 2:
                        finish(t, 0)

                    if isinstance(t, int) and t == 0:
                        link.restart()
                        (slots_of_choices, tiles_of_experts, weights_of_choices, lambda: None)[a]()

                def choices():
                    for gates, top, one in ((k.G, m1, O1), (G2, m2, O2)):
                        link(v.tensor_reduce(out=top[:], in_=gates[:], axis=AX_X, op=ALU.max))
                        link(v.tensor_tensor(tmp[:], gates[:], over_e(top), ALU.is_equal))
                        link(v.tensor_tensor(tmp[:], tmp[:], over_n(k.em8), ALU.mult))
                        link(v.tensor_reduce(out=ix[:], in_=tmp[:], axis=AX_X, op=ALU.min))
                        link(v.tensor_tensor(one[:], over_n(k.em8), over_e(ix), ALU.is_equal))
                        if one is O1:
                            link(v.scalar_tensor_tensor(out=G2[:], in0=O1[:], scalar=-3e38, in1=k.G[:], op0=ALU.mult, op1=ALU.add))
                    v.tensor_tensor(Cb[:], O1[:], O2[:], ALU.add).then_inc(s.choices, 1)
                    v.tensor_tensor(ix[:], m2[:], m1[:], ALU.subtract).then_inc(s.differ, 1)

                def slots_of_choices():
                    v.wait_ge(s.counts, 1)
                    link(v.tensor_reduce(out=cnt[:], in_=pC[:].rearrange("p n e -> p e n"), axis=AX_X, op=ALU.add))
                    link(v.tensor_scalar(cnt[:], cnt[:], float(TILE - 1), None, ALU.add))
                    link(v.tensor_copy(cnti[:], cnt[:]))
                    link(v.tensor_scalar(cnti[:], cnti[:], TILE.bit_length() - 1, None, ALU.arith_shift_right))
                    link(v.tensor_copy(cnt[:], cnti[:]))
                    link(v.tensor_copy(endf[:], cnt[:]))
                    for e in range(1, E):
                        link(v.tensor_tensor(endf[:, e:e + 1], endf[:, e - 1:e], cnt[:, e:e + 1], ALU.add))
                    link(v.tensor_tensor(startf[:], endf[:], cnt[:], ALU.subtract))
                    link(v.tensor_scalar(startf[:], startf[:], float(TILE), None, ALU.mult))
                    link(v.tensor_tensor(G2[:], pR[:], over_n(startf), ALU.add))
                    for one, pos in ((O1, k.pos1), (O2, k.pos2)):
                        link(v.tensor_tensor(tmp[:], one[:], G2[:], ALU.mult))
                        link(v.tensor_reduce(out=cntp[:], in_=tmp[:], axis=AX_X, op=ALU.add))
                        ins = v.tensor_copy(pos[:], cntp[:])
                        if one is O1:
                            link(ins)
                    ins.then_inc(s.slots, 1)

                def tiles_of_experts():
                    link(v.tensor_tensor(ge[:], view(k.tiles, 0, [1, NTILE], [0, E - 1]), view(endf, 0, [0, NTILE], [1, E - 1]), ALU.is_ge))
                    link(v.tensor_reduce(out=k.tilef[:], in_=ge[:], axis=AX_X, op=ALU.add))
                    link(v.tensor_copy(k.tilee[:], k.tilef[:]))

                def weights_of_choices():
                    v.wait_ge(s.exp, 1)
                    link(v.tensor_scalar(m2[:], ex[:], 1.0, None, ALU.add))
                    link(v.reciprocal(m1[:], m2[:]))
                    link(v.tensor_scalar(k.w1[:], m1[:], k.gt[:, 1:2], None, ALU.mult))
                    link(v.tensor_tensor(k.w2[:], k.w1[:], ex[:], ALU.mult))

                def finish(t, u):
                    link.restart()
                    v.wait_ge(s.dn, 4 * t + 2 * u + 2)
                    link(v.scalar_tensor_tensor(out=OT[:], in0=pD[u][:], scalar=k.down[:, 1:2], in1=view(k.b2s, 0, [0, 4], [1, D]),
                                                op0=ALU.mult, op1=ALU.add))
                    rows = k.X[:, bass.ds(4 * (2 * t + u), 4), :]
                    v.scalar_tensor_tensor(out=rows, in0=OT[:], scalar=k.gt[:, 1:2], in1=rows, op0=ALU.mult, op1=ALU.add).then_inc(s.x, 1)
                    v.wait_ge(s.x, 2 * t + u + 1)
                choices()
                units(v, body)
                finish(NGR // 2 - 1, 1)


def routed_experts(nc, io, k):
    with ExitStack() as ctx:
        sb = lambda n, s, d=F32: ctx.enter_context(nc.sbuf_tensor(n, s, d))
        sem = lambda n: ctx.enter_context(nc.semaphore(n))
        ps = lambda n, s, d=F32: ctx.enter_context(nc.psum_tensor(n, s, d))
        N = 6
        M = N // 2
        XR = [sb(f"XR{u}", [P, 2, ROW], I32) for u in range(N)]
        XE = [sb(f"XE{u}", [P, 2, TILE], F16) for u in range(M)]
        G32 = sb("G32", [P, NC, TILE])
        HR = [sb(f"HR{u}", [P, 2, NC, TILE], F16) for u in range(M)]
        Y = [sb(f"Y{u}", [P, 2, D]) for u in range(N)]
        pU = [ps(f"pUr{c}", [P, TILE]) for c in range(NC)]
        pD = [ps(f"pDr{u}", [P, 2, D]) for u in range(2)]
        pX = ps("pX", [P, 2, TILE], F16)
        s = Parts(**{n: sem("x_" + n) for n in "T XE up gelu hi lo dn y passed_sp passed_pool".split()})
        s.ld = [sem(f"x_ld{u}") for u in range(N)]
        s.st = [sem(f"x_st{u}") for u in range(N)]

        def tiles(eng, body, experts=False):
            def steps(i, t, count):
                es = load_experts(eng, i, min(count + 1, NTILE - i) if isinstance(i, int) else count + 1) if experts else []
                for u in range(count):
                    body(i + u, u, t, es[u:u + 2])

            full = (NTILE - 2) // N
            steps(0, 0, N)
            with eng.Fori(1, full) as t:
                steps(N * t, t, N)
            steps(N * full, full, NTILE - N * full)

        def load_experts(eng, i, count):
            _, values = nc.values_load_multi_w_load_instructions(
                k.tilee[0:1, bass.ds(i, count)], engines=[eng.engine], min_val=0, max_val=E - 1,
                skip_runtime_bounds_check_because="a sum of E - 1 comparisons")
            return values

        def more(i, n):
            return not isinstance(i, int) or i + n < NTILE

        with nc.Block() as block:
            @block.sync
            def _(sp):
                def body(i, u, t, es):
                    wait(sp, s.st[u], 32 * t)
                    if not isinstance(i, int):
                        settle(sp, s.passed_sp)
                    sp.dma_start(XR[u][:], k.xs[bass.ds(i * TILE, TILE), :].rearrange("(q p) w -> p q w", p=P)).then_inc(s.ld[u], 16)
                tiles(sp, body)

            @block.gpsimd
            def _(g):
                def body(i, u, t, es):
                    g.wait_ge(s.y, i + 1)
                    if not isinstance(i, int):
                        settle(g, s.passed_pool)
                    for q in range(2):
                        g.indirect_dma_start(k.yd, bass.IndirectOffsetOnAxis(ap=XR[u][:, q, D:ROW], axis=0), Y[u][:, q, :], None,
                                             bounds_check=2 * T - 1, oob_is_err=False).then_inc(s.st[u], 16)
                tiles(g, body)
                for u in range(N):
                    g.wait_ge(s.st[u], 32 * len(range(u, NTILE, N)))

            @block.tensor
            def _(pe):
                def transposes(i, u, t):
                    pe.wait_ge(s.ld[u], 16 * t + 16)
                    wait(pe, s.XE, i)
                    for part in range(2):
                        for q in range(2):
                            ins = pe.transpose(pX[:, part, q * P:(q + 1) * P], XR[u][:, q, part * D // 2:(part + 1) * D // 2].bitcast(F16), k.ident16[:])
                    ins.then_inc(s.T, 1)

                def up(i, u, e):
                    pe.wait_ge(s.XE, i + 1)
                    for c in range(NC):
                        wait(pe, s.gelu, NC * (i - 1) + c + 1)
                        for step, (w, part) in enumerate(((k.W1h, 0), (k.W1l, 0), (k.W1h, 1))):
                            ins = pe.matmul(pU[c][:], w[:, bass.ds(e * HID + c * P, P)], XE[u % M][:, part, :], start=(step == 0), stop=(step == 2))
                        ins.then_inc(s.up, 1)

                def down(i, u, e):
                    wait(pe, s.y, i - 1)
                    for c in range(NC):
                        if c % 2 == 0:
                            pe.wait_ge(s.lo, NC // 2 * i + c // 2 + 1)
                        for q in range(2):
                            for step, (w, part) in enumerate(((k.W2h, 0), (k.W2l, 0), (k.W2h, 1))):
                                ins = pe.matmul(pD[u % 2][:, q, :], HR[u % M][:, part, c, q * P:(q + 1) * P], w[:, bass.ds(e * HID + c * P, P)],
                                                start=(c == 0 and q == 0 and step == 0), stop=(c == NC - 1 and step == 2), skip_group_check=True)
                    ins.then_inc(s.dn, 1)

                def body(i, u, t, es):
                    if more(i, 2):
                        v, tv = ((u + 2) % N, t + (u + 2) // N)
                        transposes(i + 2, v, tv)
                    if more(i, 1):
                        up(i + 1, (u + 1) % N, es[1])
                    down(i, u, es[0])

                transposes(0, 0, 0)
                transposes(1, 1, 0)
                up(0, 0, load_experts(pe, 0, 1)[0])
                tiles(pe, body, experts=True)

            @block.scalar
            def _(act):
                def copy(i, u):
                    act.wait_ge(s.T, i + 1)
                    wait(act, s.up, NC * (i - M + 1))
                    act.activation(XE[u % M][:], pX[:], ACT.Copy).then_inc(s.XE, 1)

                def gelu(i, e):
                    for c in range(NC):
                        act.wait_ge(s.up, NC * i + c + 1)
                        wait(act, s.lo, NC // 2 * (i - 1) + c // 2 + 1)
                        act.activation(G32[:, c, :], pU[c][:], ACT.Gelu, bias=k.b1T[:, bass.ds(e * NC + c, 1)], scale=k.inv[:, 3:4]).then_inc(s.gelu, 1)

                def body(i, u, t, es):
                    if more(i, 2):
                        copy(i + 2, (u + 2) % N)
                    if more(i, 1):
                        gelu(i + 1, es[1])

                copy(0, 0)
                copy(1, 1)
                gelu(0, load_experts(act, 0, 1)[0])
                tiles(act, body, experts=True)

            @block.vector
            def _(v):
                def split(i, u):
                    for half in range(2):
                        ch = slice(2 * half, 2 * half + 2)
                        v.wait_ge(s.gelu, NC * i + 2 * half + 2)
                        wait(v, s.dn, i - M + 1)
                        v.tensor_scalar(HR[u % M][:, 0, ch, :], G32[:, ch, :], k.sc[:, 2:3], None, ALU.mult).then_inc(s.hi, 1)
                        v.wait_ge(s.hi, 2 * i + half + 1)
                        v.scalar_tensor_tensor(out=HR[u % M][:, 1, ch, :], in0=G32[:, ch, :], scalar=k.sc[:, 2:3], in1=HR[u % M][:, 0, ch, :],
                                               op0=ALU.mult, op1=ALU.subtract).then_inc(s.lo, 1)

                def result(i, u, t, e):
                    v.wait_ge(s.dn, i + 1)
                    wait(v, s.st[u], 32 * t)
                    for q in range(2):
                        ins = v.scalar_tensor_tensor(out=Y[u][:, q, :], in0=pD[u % 2][:, q, :], scalar=k.down[:, 0:1],
                                                     in1=k.b2[:, bass.ds(e * D, D)], op0=ALU.mult, op1=ALU.add)
                    ins.then_inc(s.y, 1)

                def body(i, u, t, es):
                    if more(i, 1):
                        split(i + 1, (u + 1) % N)
                    result(i, u, t, es[0])

                split(0, 0)
                tiles(v, body, experts=True)


def combine(nc, io, k):
    with ExitStack() as ctx:
        sb = lambda n, s, d=F32: ctx.enter_context(nc.sbuf_tensor(n, s, d))
        sem = lambda n: ctx.enter_context(nc.semaphore(n))
        NQ = 8
        R = NT // NQ
        YY = sb("YY", [P, 2, NT, D])
        s_ld = [sem(f"f_ld{n}") for n in range(NQ)]
        s_1, s_2, s_w, s_out = sem("f_1"), sem("f_2"), sem("f_w"), sem("f_out")
        yv = k.yd.rearrange("(c n p) d -> p c n d", c=2, p=P)
        with nc.Block() as block:
            @block.sync
            def _(sp):
                for n in range(NQ):
                    for c in range(2):
                        sp.dma_start(YY[:, c, R * n:R * n + R, :], yv[:, c, R * n:R * n + R, :]).then_inc(s_ld[n], 16)
                for n in range(NQ):
                    sp.wait_ge(s_2, n + 1)
                    sp.dma_start(io.out.rearrange("b s d -> s b d")[:, R * n:R * n + R, :], k.X[:, R * n:R * n + R, :]).then_inc(s_out, 16)
                sp.wait_ge(s_out, 16 * NQ)

            @block.scalar
            def _(a):
                for n in range(NQ):
                    a.wait_ge(s_ld[n], 32)
                    for j in range(R * n, R * n + R):
                        ins = a.activation(YY[:, 1, j, :], YY[:, 1, j, :], ACT.Copy, scale=k.w2[:, j:j + 1])
                    ins.then_inc(s_w, 1)

            @block.vector
            def _(v):
                for n in range(NQ):
                    v.wait_ge(s_ld[n], 32)
                    for j in range(R * n, R * n + R):
                        ins = v.scalar_tensor_tensor(out=k.X[:, j, :], in0=YY[:, 0, j, :], scalar=k.w1[:, j:j + 1], in1=k.X[:, j, :],
                                                     op0=ALU.mult, op1=ALU.add)
                    ins.then_inc(s_1, 1)
                    v.wait_ge(s_1, n + 1)
                    v.wait_ge(s_w, n + 1)
                    rows = slice(R * n, R * n + R)
                    v.tensor_tensor(k.X[:, rows, :], k.X[:, rows, :], YY[:, 1, rows, :], ALU.add).then_inc(s_2, 1)


INPUTS = {"x": "x", "ctx_1024": "ctx", "mask_BxS2_if1": "mask", "g_xattn": "g1", "g_ffn": "g2",
          "L0_xattn_Wq": "Wq", "L0_xattn_bq": "bq", "L0_xattn_Wk": "Wk", "L0_xattn_bk": "bk",
          "L0_xattn_Wv": "Wv", "L0_xattn_bv": "bv", "L0_xattn_Wo": "Wo", "L0_xattn_bo": "bo",
          "L0_ffn_rW": "rW", "L0_ffn_rb": "rb", "L0_ffn_W1": "W1", "L0_ffn_b1": "b1", "L0_ffn_W2": "W2", "L0_ffn_b2": "b2",
          "L0_ffn_sW1": "sW1", "L0_ffn_sb1": "sb1", "L0_ffn_sW2": "sW2", "L0_ffn_sb2": "sb2"}


def program(nc, stages=9, **io):
    io = Parts(**io)
    dram = lambda n, s, d: nc.dram_tensor(n, s, d, kind="Internal").ap()
    with ExitStack() as outer:
        def alloc(ctx, k, **tiles):
            for n, (shape, dt) in tiles.items():
                k[n] = ctx.enter_context(nc.sbuf_tensor("t_" + n, shape, dt))
        k = Parts()
        alloc(outer, k, X=([P, NT, D], F32), W1h=([P, NE * HID], F16), W1l=([P, NE * HID], F16),
              W2h=([P, NE * HID], F16), W2l=([P, NE * HID], F16),
              identf=([P, P], F32), ident16=([P, P], F16), ones=([P, P], F32), onesb=([P, P], BF16), lower=([P, P], BF16),
              b2=([P, NE * D], F32), b2s=([P, D], F32), b1T=([P, NE * NC], F32), gt=([P, 2], F32), rb=([P, E], F32),
              rW=([P, 2 * E], F16), sc=([P, 6], F32), inv=([P, 6], F32), bound=([P, 6], F32), pow2=([P, 6], F32), down=([P, 2], F32), mv=([P, NT, 2], F32),
              rstd=([P, NT], F32), nmr=([P, NT], F32))
        k.xs = dram("xs", (XS_ROWS, ROW), I32)
        k.yd = dram("yd", (2 * T, D), F32)
        k.kmd = dram("kmd", (T,), F16)
        k.s_w, k.s_empty = outer.enter_context(nc.semaphore("w_loaded")), outer.enter_context(nc.semaphore("slots_empty"))
        k.scr = [dram(f"scr{u}", (2, P, 4, W2T), F16) for u in range(NB)]
        with ExitStack() as a:
            alloc(a, k, Wq=([P, P], F32), Wk=([P, P], F32), Wv=([P, P], F32), Wo=([P, P], F32),
                  bvc=([P, 1], F32), bo=([P, D], F32), bo2=([P, D], F32), gbo=([P, D], F32), rWf=([P, E], F32), bqk=([P, 2], F32),
                  onesV=([P, 4, 4 * HD], F32), scl=([P, B], F32), mbias=([P, B], F32), b1r=([NE * NC, P], F32), padrow=([P, ROW], I32), stage1=([P, NE * HID], F32), stage2=([P, NE * HID], F32))
            k.update(Q=[], K=[], V=[], CX=[])
            k.s_c = [a.enter_context(nc.semaphore(f"a_c{u}")) for u in range(NB)]
            for u in range(NB):
                alloc(a, k, **{f"Q{u}": ([P, HD, W2T], F16), f"K{u}": ([P, H, W2T], F16), f"V{u}": ([P, 8, 4, 32], F32), f"CX{u}": ([P, 2, D], F32)})
                for n in ("Q", "K", "V", "CX"):
                    k[n].append(k[f"{n}{u}"])
            prologue(nc, io, k)
            attention(nc, io, k)
        with ExitStack() as b:
            alloc(b, k, XT=([P, 2, T], F16), w1=([P, NT], F32), w2=([P, NT], F32), tilef=([P, NTILE], F32), tilee=([P, NTILE], I32))
            with ExitStack() as c:
                alloc(c, k, PAY=([P, NT, ROW], I32), G=([P, NT, E], F32), em8=([P, E], F32), tiles=([P, NTILE], F32),
                      pos1=([P, NT], I32), pos2=([P, NT], I32))
                normalise_and_gate(nc, io, k)
                route_and_shared(nc, io, k)
            routed_experts(nc, io, k)
            combine(nc, io, k)


def kernel(**inputs):
    import numpy as np
    import concourse.bacc as bacc
    from concourse.bass_utils import run_bass_kernel_spmd

    nc = bacc.Bacc("TRN2", target_bir_lowering=False, num_devices=1)
    arrays, io = {}, {}
    for name, short in INPUTS.items():
        a = np.ascontiguousarray(inputs[name])
        arrays["in_" + short] = a
        io[short] = nc.dram_tensor("in_" + short, a.shape, mybir.dt.from_np(a.dtype), kind="ExternalInput").ap()
    io["out"] = nc.dram_tensor("out", (B, S, D), F32, kind="ExternalOutput").ap()
    program(nc, **io)
    return run_bass_kernel_spmd(nc, [arrays], core_ids=[0]).results[0]["out"]
```
